# Optimizing a Trainium2 kernel written in Bass

```python
import numpy as np
import jax
import jax.numpy as jnp

def _softmax(x, axis=-1):
    return jax.nn.softmax(x, axis=axis)

def _gelu(x):
    return jax.nn.gelu(x, approximate=True)

def _silu(x):
    return jax.nn.silu(x)

def _sigmoid(x):
    return jax.nn.sigmoid(x)

def _layernorm(x, axis=-1, eps=1e-05):
    m = jnp.mean(x, axis=axis, keepdims=True)
    v = jnp.var(x, axis=axis, keepdims=True)
    return (x - m) / jnp.sqrt(v + eps)

def _scatter_add(tgt, idx, src, axis=0):
    return tgt.at[idx].add(src)

def _segment_sum(src, seg, n):
    return jax.ops.segment_sum(src, seg, n)
kernel_name = 'mk_hybrid_d1_jaxref_r8_db9910'

def setup_inputs(seed: int=0):
    np.random.seed(seed)
    _w = jnp.asarray

    def _L0_attn_a_setup():
        import jax, jax.numpy as jnp
        import numpy as np
        D_MODEL = 256
        NUM_HEADS = 16
        DK = D_MODEL // NUM_HEADS
        key = jax.random.key(seed)
        kx, kq, kk, kv, ko = jax.random.split(key, 5)
        s = 1.0 / np.sqrt(D_MODEL)
        return {'x': jax.random.normal(kx, (4, 256, D_MODEL), dtype=jnp.float32), 'Wq': jax.random.normal(kq, (D_MODEL, D_MODEL), dtype=jnp.float32) * s, 'Wk': jax.random.normal(kk, (D_MODEL, D_MODEL), dtype=jnp.float32) * s, 'Wv': jax.random.normal(kv, (D_MODEL, D_MODEL), dtype=jnp.float32) * s, 'Wo': jax.random.normal(ko, (D_MODEL, D_MODEL), dtype=jnp.float32) * s}
    _L0_attn_a_in = _L0_attn_a_setup()

    def _L0_attn_b_setup():
        import jax, jax.numpy as jnp
        import numpy as np
        B, L, H, NH = (2, 256, 256, 16)
        K = H // NH
        EPS = 1e-05
        SCALE = K ** (-0.5)

        def _gla(q, k, v, g):

            def step(S, xs):
                q_t, k_t, v_t, g_t = xs
                S = jnp.exp(g_t)[:, :, None] * S + k_t[:, :, None] * v_t[:, None, :]
                o_t = jnp.einsum('bk,bkv->bv', q_t, S)
                return (S, o_t)
            S0 = jnp.zeros((q.shape[0], q.shape[2], v.shape[2]), dtype=q.dtype)
            xs = (jnp.swapaxes(q, 0, 1), jnp.swapaxes(k, 0, 1), jnp.swapaxes(v, 0, 1), jnp.swapaxes(g, 0, 1))
            _, o = jax.lax.scan(step, S0, xs)
            return jnp.swapaxes(o, 0, 1)
        key = jax.random.key(seed)
        k0, k1, k2, k3, k4 = jax.random.split(key, 5)
        std = 0.02
        return {'hidden_states': jax.random.normal(k0, (B, L, H), dtype=jnp.float32), 'Wq': jax.random.normal(k1, (K, H), dtype=jnp.float32) * std, 'Wk': jax.random.normal(k2, (K, H), dtype=jnp.float32) * std, 'Wog': jax.random.normal(k3, (H, H), dtype=jnp.float32) * std, 'Wig': jax.random.normal(k4, (H, H), dtype=jnp.float32) * std, 'g_weight': jnp.ones((H,), dtype=jnp.float32)}
    _L0_attn_b_in = _L0_attn_b_setup()

    def _L0_ffn_setup():
        import jax, jax.numpy as jnp
        import numpy as np
        HIDDEN = 256
        INTER = 1024
        COMPRESSION = 128.9

        def _n_ctrl(out_size, in_size):
            return max(16, int(out_size * in_size / COMPRESSION))

        def _catmull_rom_grid(n_ctrl, n_samples):
            t = np.linspace(0.0, n_ctrl - 1.0, n_samples, dtype=np.float64)
            i = np.clip(np.floor(t).astype(np.int64), 0, n_ctrl - 2)
            f = (t - i).astype(np.float32)
            idx = np.stack([np.clip(i + k, 0, n_ctrl - 1) for k in (-1, 0, 1, 2)], axis=0)
            return (jnp.asarray(idx.astype(np.int32)), jnp.asarray(f))

        def spline_reconstruct(control_points, out_size, in_size):
            n = out_size * in_size
            idx, f = _catmull_rom_grid(control_points.shape[0], n)
            p0, p1, p2, p3 = (control_points[idx[0]], control_points[idx[1]], control_points[idx[2]], control_points[idx[3]])
            f2 = f * f
            f3 = f2 * f
            w = 0.5 * (2.0 * p1 + (p2 - p0) * f + (2.0 * p0 - 5.0 * p1 + 4.0 * p2 - p3) * f2 + (3.0 * p1 - p0 - 3.0 * p2 + p3) * f3)
            return w.reshape(out_size, in_size)
        key = jax.random.key(seed)
        k0, k1, k2, k3 = jax.random.split(key, 4)
        hidden_states = jax.random.normal(k0, (4, 256, HIDDEN), dtype=jnp.float32)
        gate_cp = jax.random.normal(k1, (_n_ctrl(INTER, HIDDEN),), dtype=jnp.float32) * 0.02
        up_cp = jax.random.normal(k2, (_n_ctrl(INTER, HIDDEN),), dtype=jnp.float32) * 0.02
        down_cp = jax.random.normal(k3, (_n_ctrl(HIDDEN, INTER),), dtype=jnp.float32) * 0.02
        return {'hidden_states': hidden_states, 'gate_cp': gate_cp, 'up_cp': up_cp, 'down_cp': down_cp}
    _L0_ffn_in = _L0_ffn_setup()
    _d = {'L0_attn_a_x': _L0_attn_a_in['x'], 'L0_attn_a_Wq': _L0_attn_a_in['Wq'], 'L0_attn_a_Wk': _L0_attn_a_in['Wk'], 'L0_attn_a_Wv': _L0_attn_a_in['Wv'], 'L0_attn_a_Wo': _L0_attn_a_in['Wo'], 'L0_attn_b_Wq': _L0_attn_b_in['Wq'], 'L0_attn_b_Wk': _L0_attn_b_in['Wk'], 'L0_attn_b_Wog': _L0_attn_b_in['Wog'], 'L0_attn_b_Wig': _L0_attn_b_in['Wig'], 'L0_attn_b_g_weight': _L0_attn_b_in['g_weight'], 'L0_ffn_gate_cp': _L0_ffn_in['gate_cp'], 'L0_ffn_up_cp': _L0_ffn_in['up_cp'], 'L0_ffn_down_cp': _L0_ffn_in['down_cp']}
    _x0 = _d['L0_attn_a_x']
    _d['L0_attn_a_x'] = jax.random.normal(jax.random.fold_in(jax.random.key(seed), 1), (16, 256, 256), dtype=_x0.dtype)
    del _x0
    return _d

def reference(L0_attn_a_x, L0_attn_a_Wq, L0_attn_a_Wk, L0_attn_a_Wv, L0_attn_a_Wo, L0_attn_b_Wq, L0_attn_b_Wk, L0_attn_b_Wog, L0_attn_b_Wig, L0_attn_b_g_weight, L0_ffn_gate_cp, L0_ffn_up_cp, L0_ffn_down_cp):

    def _L0_attn_a_ref(x, Wq, Wk, Wv, Wo):
        import jax, jax.numpy as jnp
        import numpy as np
        D_MODEL = 256
        NUM_HEADS = 16
        DK = D_MODEL // NUM_HEADS
        B, S, D = x.shape
        H, dk = (NUM_HEADS, DK)
        q = (x @ Wq.T).reshape(B, S, H, dk).transpose(0, 2, 1, 3)
        k = (x @ Wk.T).reshape(B, S, H, dk).transpose(0, 2, 1, 3)
        v = (x @ Wv.T).reshape(B, S, H, dk).transpose(0, 2, 1, 3)
        scores = jnp.einsum('bhqd,bhkd->bhqk', q, k) / jnp.sqrt(jnp.float32(dk))
        causal = jnp.tril(jnp.ones((S, S), dtype=bool))
        scores = jnp.where(causal, scores, jnp.finfo(scores.dtype).min)
        probs = jax.nn.softmax(scores, axis=-1)
        attn = jnp.einsum('bhqk,bhkd->bhqd', probs, v)
        attn = attn.transpose(0, 2, 1, 3).reshape(B, S, D)
        return attn @ Wo.T

    def _L0_attn_b_ref(hidden_states, Wq, Wk, Wog, Wig, g_weight):
        import jax, jax.numpy as jnp
        import numpy as np
        B, L, H, NH = (2, 256, 256, 16)
        K = H // NH
        EPS = 1e-05
        SCALE = K ** (-0.5)

        def _gla(q, k, v, g):

            def step(S, xs):
                q_t, k_t, v_t, g_t = xs
                S = jnp.exp(g_t)[:, :, None] * S + k_t[:, :, None] * v_t[:, None, :]
                o_t = jnp.einsum('bk,bkv->bv', q_t, S)
                return (S, o_t)
            S0 = jnp.zeros((q.shape[0], q.shape[2], v.shape[2]), dtype=q.dtype)
            xs = (jnp.swapaxes(q, 0, 1), jnp.swapaxes(k, 0, 1), jnp.swapaxes(v, 0, 1), jnp.swapaxes(g, 0, 1))
            _, o = jax.lax.scan(step, S0, xs)
            return jnp.swapaxes(o, 0, 1)
        x = hidden_states
        q = x @ Wq.T
        k_sig = jax.nn.sigmoid(x @ Wk.T)
        q = jax.nn.silu(q) * SCALE
        gf = jax.nn.log_sigmoid(-k_sig)
        o = _gla(q, k_sig, x, gf)
        go = o @ Wog.T + x @ Wig.T
        rms = o * jax.lax.rsqrt(jnp.mean(o * o, axis=-1, keepdims=True) + EPS) * g_weight
        return rms * go * jax.nn.sigmoid(go)

    def _L0_ffn_ref(hidden_states, gate_cp, up_cp, down_cp):
        import jax, jax.numpy as jnp
        import numpy as np
        HIDDEN = 256
        INTER = 1024
        COMPRESSION = 128.9

        def _n_ctrl(out_size, in_size):
            return max(16, int(out_size * in_size / COMPRESSION))

        def _catmull_rom_grid(n_ctrl, n_samples):
            t = np.linspace(0.0, n_ctrl - 1.0, n_samples, dtype=np.float64)
            i = np.clip(np.floor(t).astype(np.int64), 0, n_ctrl - 2)
            f = (t - i).astype(np.float32)
            idx = np.stack([np.clip(i + k, 0, n_ctrl - 1) for k in (-1, 0, 1, 2)], axis=0)
            return (jnp.asarray(idx.astype(np.int32)), jnp.asarray(f))

        def spline_reconstruct(control_points, out_size, in_size):
            n = out_size * in_size
            idx, f = _catmull_rom_grid(control_points.shape[0], n)
            p0, p1, p2, p3 = (control_points[idx[0]], control_points[idx[1]], control_points[idx[2]], control_points[idx[3]])
            f2 = f * f
            f3 = f2 * f
            w = 0.5 * (2.0 * p1 + (p2 - p0) * f + (2.0 * p0 - 5.0 * p1 + 4.0 * p2 - p3) * f2 + (3.0 * p1 - p0 - 3.0 * p2 + p3) * f3)
            return w.reshape(out_size, in_size)
        gate_w = spline_reconstruct(gate_cp, INTER, HIDDEN)
        up_w = spline_reconstruct(up_cp, INTER, HIDDEN)
        down_w = spline_reconstruct(down_cp, HIDDEN, INTER)
        gate = jnp.einsum('bsh,ih->bsi', hidden_states, gate_w)
        up = jnp.einsum('bsh,ih->bsi', hidden_states, up_w)
        inter = jax.nn.silu(gate) * up
        return jnp.einsum('bsi,hi->bsh', inter, down_w)
    x = L0_attn_a_x
    x = x + _L0_attn_a_ref(_layernorm(x, axis=-1), L0_attn_a_Wq, L0_attn_a_Wk, L0_attn_a_Wv, L0_attn_a_Wo)
    x = x + _L0_ffn_ref(_layernorm(x, axis=-1), L0_ffn_gate_cp, L0_ffn_up_cp, L0_ffn_down_cp)
    x = x + _L0_attn_b_ref(_layernorm(x, axis=-1), L0_attn_b_Wq, L0_attn_b_Wk, L0_attn_b_Wog, L0_attn_b_Wig, L0_attn_b_g_weight)
    x = x + _L0_ffn_ref(_layernorm(x, axis=-1), L0_ffn_gate_cp, L0_ffn_up_cp, L0_ffn_down_cp)
    return x

_drawn_inputs = setup_inputs


def setup_inputs(seed=0):
    import zlib

    import numpy as np

    out = dict(_drawn_inputs(seed))
    spreads = {'L0_attn_b_g_weight': (1.0, 0.2)}
    factors = {'L0_attn_b_Wog': 2.934}
    for name, (base, spread) in spreads.items():
        noise = np.random.default_rng([zlib.crc32(name.encode()), seed]).standard_normal(out[name].shape)
        drawn = base * np.exp(spread * noise) if base else spread * noise
        out[name] = jnp.asarray(drawn.astype(out[name].dtype))
    for name, factor in factors.items():
        out[name] = (out[name] * factor).astype(out[name].dtype)
    return out
```

```python
from contextlib import ExitStack

import numpy as np

import concourse.bass as bass
from concourse import mybir

ACT = mybir.ActivationFunctionType
ALU = mybir.AluOpType
AX = mybir.AxisListType
F32 = mybir.dt.float32
F32R = mybir.dt.float32r
BF16 = mybir.dt.bfloat16

P = 128
B = 16
S = 256
D = 256
NT = B * S // P
TB = S // P
CT = D // P
H = 16
DK = D // H
HH = 8
NP = H // 2
EPS = 1e-5
NEG = -3.0e38
INTER = 1024
MT = INTER // P
N_CTRL = 2033
WIN = 6
FRONT = 2
BACK = 3
N_CP = FRONT + N_CTRL + BACK
KG = 16
NG = 7
GR = NG * KG
GROW = 2.0 ** 60
BIG = 3.0e38
LEAD = 2

K_S = 65
K_ST = 67
ZROW = 64
MROW = 65


class Signals:
    pass


def spline_basis():
    n = INTER * D
    t = np.linspace(0.0, N_CTRL - 1.0, n, dtype=np.float64)
    i = np.clip(np.floor(t).astype(np.int64), 0, N_CTRL - 2)
    f = (t - i).astype(np.float32).astype(np.float64)
    coef = [
        0.5 * (-f + 2 * f * f - f * f * f),
        0.5 * (2 - 5 * f * f + 3 * f * f * f),
        0.5 * (f + 4 * f * f - 3 * f * f * f),
        0.5 * (-f * f + f * f * f),
    ]
    rows = np.arange(n) // D
    base = 127 * (rows // 64) + 2 * (rows % 64) - FRONT
    phi = np.zeros((n, WIN))
    for k in range(4):
        m = np.clip(i + k - 1, 0, N_CTRL - 1) - base
        assert m.min() >= 0 and m.max() < WIN
        np.add.at(phi, (np.arange(n), m), coef[k])
    phi = phi.reshape(MT, P, D, WIN).transpose(0, 1, 3, 2)
    return np.ascontiguousarray(phi.reshape(MT, P, WIN * D).astype(np.float32))


def decay_windows():
    w = np.zeros((GR, 6, S), np.float32)
    run, start, krun, kstart, qwin, kwin = (w[:, n] for n in range(6))
    for g in range(4):
        r = slice(KG * g, KG * g + KG)
        run[r] = 1.0
        run[r, ::64] = 0.0
        start[r, ::64] = GROW
        qwin[r, 64 * g:64 * g + 64] = 1.0
        kwin[r, 64 * g:64 * g + 64] = KG ** -0.5
    for g, ref, length in ((4, 64, 64), (5, 192, 64), (6, 128, 128)):
        r = slice(KG * g, KG * g + KG)
        run[r, ref + 1:ref + length] = 1.0
        start[r, ref] = 1.0
        krun[r, ref - length:ref] = 1.0
        kstart[r, ref] = 1.0
        qwin[r, ref:ref + length] = 1.0
        kwin[r, ref - length:ref] = KG ** -0.5
    return w


def build(nc, x, a_wq, a_wk, a_wv, a_wo, b_wq, b_wk, b_wog, b_wig, g_weight, cps, phi, windows, out):
    outer = ExitStack()
    with outer:
        def sb(name, shape, dt, where=outer):
            return where.enter_context(nc.sbuf_tensor(name, shape, dt))

        sems = {}

        def sem(name):
            sems[name] = outer.enter_context(nc.semaphore(name))
            return sems[name]

        bank = [outer.enter_context(nc.psum_tensor(f"bank{n}", [P, 512], F32)) for n in range(4)]
        pair_a = outer.enter_context(nc.psum_tensor("pair_a", [P, 2, 512], F32))
        pair_b = outer.enter_context(nc.psum_tensor("pair_b", [P, 2, 512], F32))
        bank_t, bank_p, bank_o, bank_y = bank
        prep_bank = bank + [pair_a[:, 0], pair_a[:, 1], pair_b[:, 0], pair_b[:, 1]]

        X = sb("X", [P, NT, D], F32)
        ident = sb("ident", [P, P], F32)
        ident16 = sb("ident16", [P, P], BF16)
        causal_neg = sb("causal_neg", [P, 2, P], BF16)
        half_neg = sb("half_neg", [P, 2, TB], F32)
        wog = sb("wog_hi", [P, CT, D], F32R), sb("wog_lo", [P, CT, D], F32R)
        wig = sb("wig_hi", [P, CT, D], F32R), sb("wig_lo", [P, CT, D], F32R)
        wqk_hi = sb("wqk_hi", [P, 2, CT, GR], F32R)
        wqk_lo = sb("wqk_lo", [P, 2, CT, GR], F32R)
        st = sb("st", [P, 2, TB, 6], F32)
        mv = sb("mv", [P, 2, TB, 2], F32)
        ve = sb("ve", [P, 2, TB], F32)
        rs = sb("rs", [P, 2, TB], F32)
        spline = sb("spline", [P, 3 * MT, D], F32)
        wnat = spline[:, 0:6 * CT, :].rearrange("p (w o) c -> p w o c", w=6)
        bnat = spline[0:KG, 6 * CT:6 * CT + 2, :]

        with ExitStack() as at:
            wq, wk, wv, wo = ((sb(n + "_hi", [P, CT, D], F32R, at), sb(n + "_lo", [P, CT, D], F32R, at))
                              for n in ("wq", "wk", "wv", "wo"))
            cpw = sb("cpw", [P, 3, MT, WIN], F32, at)
            basis = sb("basis", [P, 2, WIN, P], F32, at)
            prod = sb("prod", [P, WIN, P], F32, at)
            xn = sb("xn", [P, TB, D], F32, at)
            xT_hi = sb("xT_hi", [P, 2, CT, S], F32R, at)
            xT_lo = sb("xT_lo", [P, 2, CT, S], F32R, at)
            stage = sb("stage", [P, 2, 4, S], F32R, at)
            stack = sb("stack", [K_ST, 2, 2, 2, HH, S], F32R, at)
            V = sb("V", [P, 2, TB, H, 32], F32, at)
            mx = sb("mx", [P, 2, HH, 3], F32, at)
            mx2 = sb("mx2", [P, 2, TB, HH], F32, at)
            mrow = sb("mrow", [HH, 2, 2, S], F32R, at)
            prob = sb("prob", [P, 2, 2, 3 * P], F32, at)
            oT = sb("oT", [P, 2, 2, S], F32, at)
            rden = sb("rden", [P, 2, TB, HH], F32, at)
            att = sb("att", [P, TB, D], F32, at)
            attT_hi = sb("attT_hi", [P, CT, S], F32R, at)
            attT_lo = sb("attT_lo", [P, CT, S], F32R, at)

        with ExitStack() as ft:
            wg_hi = sb("wg_hi", [P, CT, INTER], F32R, ft)
            wg_lo = sb("wg_lo", [P, CT, INTER], F32R, ft)
            wu_hi = sb("wu_hi", [P, CT, INTER], F32R, ft)
            wu_lo = sb("wu_lo", [P, CT, INTER], F32R, ft)
            wd_hi = sb("wd_hi", [P, MT, D], F32R, ft)
            wd_lo = sb("wd_lo", [P, MT, D], F32R, ft)
            xn_f = sb("xn_f", [P, 2 * TB, D], F32, ft)
            fT_hi = sb("fT_hi", [P, 2, CT, 2 * S], F32R, ft)
            fT_lo = sb("fT_lo", [P, 2, CT, 2 * S], F32R, ft)
            gact = sb("gact", [P, 2, 2 * S], F32, ft)
            inter = sb("inter", [P, 2, 2 * S], F32, ft)
            in_hi = sb("in_hi", [P, 2, 2 * S], F32R, ft)
            in_lo = sb("in_lo", [P, 2, 2 * S], F32R, ft)
            yT = sb("yT", [P, CT, 2 * S], F32, ft)
            causal01 = sb("causal01", [P, TB, S], F32, ft)
            gw_row = sb("gw_row", [P, D], F32, ft)
            win = sb("win", [GR, 6, S], F32, ft)
            gx_hi = sb("gx_hi", [P, 2, TB, D], F32R, ft)
            gx_lo = sb("gx_lo", [P, 2, TB, D], F32R, ft)
            gT_hi = sb("gT_hi", [P, 2, CT, S], F32R, ft)
            gT_lo = sb("gT_lo", [P, 2, CT, S], F32R, ft)
            qk_hi = sb("qk_hi", [GR, 2, S], F32R, ft)
            qk_lo = sb("qk_lo", [GR, 2, S], F32R, ft)
            am_hi = sb("am_hi", [P, TB, S], F32R, ft)
            am_lo = sb("am_lo", [P, TB, S], F32R, ft)
            goT_hi = sb("goT_hi", [P, CT, S], F32R, ft)
            goT_lo = sb("goT_lo", [P, CT, S], F32R, ft)
            junk = sb("junk", [P, D], F32, ft)
            ssq = sb("ssq", [P, TB], F32, ft)
            vs = sb("vs", [P, TB], F32, ft)
            rr = sb("rr", [P, TB], F32, ft)
        row = iter(range(3 * MT))

        def gwork(n, parts=P):
            r = next(row)
            for _ in range(n - 1):
                next(row)
            return spline[0:parts, r:r + n, :]

        gx, am, rms, gsig, gout, gmul = (gwork(2) for _ in range(6))
        sig, qk = gwork(2, GR), gwork(2, GR)
        dec, qsig, kwn, dq, dk, qsil, fq, fk = (gwork(1, GR)[:, 0] for _ in range(8))

        heads = nc.dram_tensor("heads", [2, 2, 4, HH, DK, S], F32, kind="Internal").ap()

        s_x = [sem(f"x_loaded{n}") for n in range(3)]
        s_w = sem("weights_loaded")
        s_cp = sem("control_points_loaded")
        s_ident = sem("ident_made")
        s_const = sem("constants_made")
        s_prep_ps, s_prep_hi, s_prep_lo = sem("prep_turned"), sem("prep_high"), sem("prep_low")
        s_fturn, s_fhi, s_flo = sem("spline_turned"), sem("spline_high"), sem("spline_low")
        s_gc, s_gload = sem("gla_constants_made"), sem("gla_constants_loaded")
        per = {}

        def counted(name, n):
            s = sem(name)
            per[s.name] = n
            return s

        a_bn, a_mv, a_ve = counted("a_bn", 2), counted("a_mv", 2), counted("a_ve", 1)
        a_xn = counted("a_xn", 2)
        a_xl = counted("a_xl", 1)
        a_qkl = counted("a_qkl", 2)
        a_mx = counted("a_mx", NP)
        a_m = counted("a_m", 4)
        a_mh, a_ml = counted("a_mh", 2), counted("a_ml", 2)
        a_rd, a_at = counted("a_rd", 2), counted("a_at", 2)
        a_atl = counted("a_atl", 1)
        a_res = counted("a_res", 1)
        by_dve = [a_bn, a_mv, a_ve, a_xn, a_xl, a_qkl, a_mx, a_m, a_mh, a_ml, a_rd, a_at, a_atl, a_res]
        a_rs, a_pm = counted("a_rs", 1), counted("a_pm", NP)
        a_sp4 = counted("a_spl", 12)
        by_pool = [a_rs, a_pm, a_sp4]
        a_xh, a_qkh = counted("a_xh", 1), counted("a_qkh", 2)
        a_v, a_e = counted("a_v", 1), counted("a_e", NP)
        a_o, a_ath = counted("a_o", 2), counted("a_ath", 1)
        by_act = [a_xh, a_qkh, a_v, a_e, a_o, a_ath]
        a_xT, a_qkp, a_vp = counted("a_xT", 1), counted("a_qkp", 2), counted("a_vp", 1)
        a_sp, a_mT, a_stp = counted("a_sp", NP), counted("a_mT", 2), counted("a_stp", NP)
        a_pv, a_ot, a_atT, a_y = counted("a_pv", NP), counted("a_ot", 2), counted("a_atT", 1), counted("a_y", 1)
        by_pe = [a_xT, a_qkp, a_vp, a_sp, a_mT, a_stp, a_pv, a_ot, a_atT, a_y]
        N_STACK = 4
        a_wr = [counted(f"a_wr{h}", 16) for h in range(2)]
        a_stk = [counted(f"a_stk{h}", 16 * N_STACK) for h in range(2)]
        a_md = [counted(f"a_md{h}", 32) for h in range(2)]
        a_phi = counted("a_phi", 16)
        passed_dve, passed_pool, passed_sp = sem("passed_dve"), sem("passed_pool"), sem("passed_sp")
        s_out = sem("out_stored")

        def ffn_semaphores(tag):
            f = Signals()

            def own(n, count):
                return counted(f"{tag}_{n}", count)

            f.bn, f.mv, f.ve, f.xn, f.xl = own("bn", 4), own("mv", 4), own("ve", 1), own("xn", 4), own("xl", 2)
            f.up, f.il, f.res = own("up", MT), own("il", MT), own("res", 2)
            f.dve = [f.bn, f.mv, f.ve, f.xn, f.xl, f.up, f.il, f.res]
            f.rs = own("rs", 1)
            f.pool = [f.rs]
            f.xh, f.si, f.ih, f.yc = own("xh", 2), own("si", MT), own("ih", MT), own("yc", 2)
            f.act = [f.xh, f.si, f.ih, f.yc]
            f.xT, f.gp, f.upp, f.dp, f.yT = own("xT", 2), own("gp", MT), own("upp", MT), own("dp", MT), own("yT", 2)
            f.pe = [f.xT, f.gp, f.upp, f.dp, f.yT]
            return f

        f1, f2 = ffn_semaphores("f1"), ffn_semaphores("f2")

        def gla_semaphores():
            f = Signals()

            def own(n, count=1):
                return counted(f"g_{n}", count)

            f.bn, f.mv, f.ve, f.xn, f.xl, f.qs = own("bn", 2), own("mv", 2), own("ve"), own("xn", 2), own("xl"), own("qs")
            f.sf, f.rc, f.sb, f.qd, f.kd, f.qkl = own("sf"), own("rc"), own("sb"), own("qd"), own("kd"), own("qkl")
            f.am, f.aml, f.gol, f.vs, f.gm = own("am"), own("aml"), own("gol"), own("vs"), own("gm")
            f.dve = [f.bn, f.mv, f.ve, f.xn, f.xl, f.qs, f.sf, f.rc, f.sb, f.qd, f.kd, f.qkl, f.am, f.aml, f.gol,
                     f.vs, f.gm]
            f.rs, f.gl, f.w, f.rr, f.mu, f.res = own("rs"), own("gl"), own("w", 4), own("rr"), own("mu", 2), own("res")
            f.pool = [f.rs, f.gl, f.w, f.rr, f.mu, f.res]
            f.xh, f.gh, f.sg, f.de, f.qkh, f.amh = own("xh"), own("gh"), own("sg"), own("de"), own("qkh"), own("amh")
            f.goh, f.sq, f.rm, f.gs = own("goh"), own("sq", 2), own("rm", 2), own("gs")
            f.act = [f.xh, f.gh, f.sg, f.de, f.qkh, f.amh, f.goh, f.sq, f.rm, f.gs]
            f.xT, f.qk, f.ap, f.go1, f.oT, f.ot, f.go = (own(n) for n in ("xT", "qk", "ap", "go1", "oT", "ot", "go"))
            f.pe = [f.xT, f.qk, f.ap, f.go1, f.oT, f.ot, f.go]
            return f

        g_ = gla_semaphores()

        def lead(eng, owned):
            for s in owned:
                eng.sem_inc(s, LEAD * per[s.name])

        def upto(s, b, k):
            return per[s.name] * (b + LEAD) + k

        def mm3(pe, dst, l_hi, l_lo, r_hi, r_lo, first, last):
            pe.matmul(dst, l_hi, r_hi, start=first, stop=False)
            pe.matmul(dst, l_hi, r_lo, start=False, stop=False)
            return pe.matmul(dst, l_lo, r_hi, start=False, stop=last)

        phi_t = phi.rearrange("j p (m c) -> j p m c", m=WIN)
        x_t = x.rearrange("b (t p) c -> p (b t) c", p=P)
        out_t = out.rearrange("b (t p) c -> p (b t) c", p=P)
        bank_y4 = bank_y[:, :].rearrange("p (t h w) -> p t h w", t=TB, h=HH)
        def run_periods(eng, period):
            period(0, 0, 0, prev=False)
            period(1, 0, 1)
            with eng.Fori(1, B // 2 - 2) as j:
                period(2 * j, j, 0)
                period(2 * j + 1, j, 1)
            period(B - 4, B // 2 - 2, 0)
            period(B - 3, B // 2 - 2, 1, nxt3=False)
            period(B - 2, B // 2 - 1, 0, nxt2=False, nxt3=False)
            period(B - 1, B // 2 - 1, 1, nxt=False, nxt2=False, nxt3=False)

        PAIRS = B // 2

        def run_pairs(period):
            def run(eng):
                period(0, 0, prev=False)
                with eng.Fori(0, PAIRS // 2 - 1) as j:
                    period(2 * j + 1, 1)
                    period(2 * j + 2, 0)
                period(PAIRS - 1, 1, nxt=False)
            return run

        def run_gla(eng, period):
            period(0, 0, prev=False)
            with eng.Fori(0, B // 2 - 2) as j:
                period(2 * j + 1, 1)
                period(2 * j + 2, 0)
            period(B - 3, 1)
            period(B - 2, 0, nxt2=False)
            period(B - 1, 1, nxt2=False, nxt=False)
            period(B, 0, nxt2=False, nxt=False, cur=False)

        def turned_down(t):
            return t.rearrange("p (c x q) -> p c q x", c=CT, q=4)

        block = outer.enter_context(nc.Block())

        @block.sync
        def _(sp):
            sp.dma_start(X[:, 0:TB, :], x_t[:, 0:TB, :]).then_inc(s_x[0], 16)
            for n, w in enumerate((a_wq, a_wk, a_wv, a_wo, b_wog, b_wig)):
                sp.dma_start(wnat[:, n], w.rearrange("(o p) c -> p o c", p=P)).then_inc(s_w, 16)
            for n, w in enumerate((b_wq, b_wk)):
                sp.dma_start(bnat[:, n, :], w).then_inc(s_w, 16)
            sp.dma_start(X[:, TB:2 * TB, :], x_t[:, TB:2 * TB, :]).then_inc(s_x[1], 16)
            sp.dma_start(basis[:, 0], phi_t[0, :, :, 0:P]).then_inc(a_phi, 16)
            for w in range(3):
                for half in range(2):
                    window = bass.AP(tensor=cps.tensor, offset=w * N_CP + 127 * half,
                                     ap=[[2, 64], [254, MT], [1, WIN]])
                    sp.dma_start(cpw[64 * half:64 * half + 64, w], window).then_inc(s_cp, 16)
            sp.dma_start(X[:, 2 * TB:, :], x_t[:, 2 * TB:, :]).then_inc(s_x[2], 16)
            lead(sp, a_stk + a_md + a_wr + [a_phi])

            def stack_half(b, u, h, after_use=True):
                sp.wait_ge(a_qkh, upto(a_qkh, b, h + 1))
                sp.sem_inc(passed_sp, 1)
                sp.wait_ge(a_qkl, upto(a_qkl, b, h + 1))
                sp.sem_inc(passed_sp, 1)
                if after_use:
                    sp.wait_ge(a_stp, upto(a_stp, b - 2, 4 * h + 4))
                sp.dma_start(heads[u, h].rearrange("n h d t -> (h d) n t"),
                             stage[:, h].bitcast(F32)).then_inc(a_wr[h], 16)
                sp.wait_ge(a_wr[h], upto(a_wr[h], b, 16))
                for r in range(2):
                    sp.dma_start(stack[DK * r:DK * r + DK, u, h].bitcast(F32),
                                 heads[u, h, 2 * r:2 * r + 2].rearrange("n h d t -> d (n h) t")).then_inc(a_stk[h], 16)
                for n in range(2):
                    sp.dma_start(stack[2 * DK:3 * DK, u, h, n].bitcast(F32),
                                 heads[u, h, 3 * n].rearrange("h d t -> d h t")).then_inc(a_stk[h], 16)

            def max_rows(b, u, h):
                sp.wait_ge(a_ml, upto(a_ml, b, h + 1))
                for n in range(2):
                    sp.dma_start(stack[MROW + n:MROW + n + 1, u, h, 0, :, :].bitcast(F32),
                                 mrow[:, h, n, :].bitcast(F32)).then_inc(a_md[h], 16)

            sp.wait_ge(s_const, 3)
            for b in range(2):
                stack_half(b, b, 0, False)
                stack_half(b, b, 1, False)
            max_rows(0, 0, 0)

            def period(b, j, u, prev=True, nxt=True, nxt2=True, nxt3=True):
                max_rows(b, u, 1)
                if nxt:
                    sp.wait_ge(a_sp4, upto(a_sp4, b - 1, 12))
                    sp.sem_inc(passed_sp, 1)
                    tile = j + u
                    sp.dma_start(basis[:, 1 - u], phi_t[bass.ds(tile, 1), :, :, (1 - u) * P:(1 - u) * P + P]
                                 .rearrange("j p m c -> (j p) m c")).then_inc(a_phi, 16)
                if nxt2:
                    stack_half(b + 2, u, 0)
                if nxt:
                    max_rows(b + 1, 1 - u, 0)
                if nxt2:
                    stack_half(b + 2, u, 1)

            run_periods(sp, period)
            sp.wait_ge(s_fturn, 1)
            sp.dma_start(gw_row[:, :], g_weight.rearrange("(o c) -> o c", o=1).to_broadcast([P, D])
                         ).then_inc(s_gload, 16)
            sp.dma_start(win[:, :, :], windows).then_inc(s_gload, 16)
            with sp.Fori(0, PAIRS) as g:
                sp.wait_ge(f2.res, upto(f2.res, g, 2))
                sp.dma_start(out_t[:, bass.ds(2 * TB * g, 2 * TB), :],
                             X[:, bass.ds(2 * TB * g, 2 * TB), :]).then_inc(s_out, 16)
            sp.wait_ge(s_out, 16 * PAIRS)

        @block.gpsimd
        def _(pool):
            pool.memset(ident[:, :], 0.0).then_inc(s_ident, 1)
            pool.wait_ge(s_ident, 1)
            pool.affine_select(out=ident[:, :], in_=ident[:, :], compare_op=ALU.not_equal, fill=1.0, base=0,
                               pattern=[[-1, P]], channel_multiplier=1).then_inc(s_ident, 1)
            lead(pool, by_pool + f1.pool + f2.pool + g_.pool)
            pool.wait_ge(s_ident, 2)
            pool.memset(stack[64:K_ST, :, :, 0].bitcast(F32), 0.0).then_inc(s_const, 1)
            pool.memset(stack[64:K_ST, :, :, 1].bitcast(F32), 1.0).then_inc(s_const, 1)
            pool.wait_ge(s_const, 2)
            pool.memset(stack[32:64].bitcast(F32), 0.0).then_inc(s_const, 1)
            pool.wait_ge(s_const, 3)
            pool.memset(causal_neg[:, :, :], 0.0).then_inc(s_const, 1)
            pool.memset(half_neg[:, :, :], -0.5).then_inc(s_const, 1)
            pool.memset(V[:, :, :, :, DK:DK + 1], 1.0).then_inc(s_const, 1)
            pool.memset(V[:, :, :, :, DK + 1:32], 0.0).then_inc(s_const, 1)
            pool.wait_ge(s_const, 7)
            pool.affine_select(out=causal_neg[:, :, :], in_=causal_neg[:, :, :], compare_op=ALU.is_ge,
                               fill=NEG, base=0, pattern=[[0, 2], [-1, P]],
                               channel_multiplier=1).then_inc(s_const, 1)
            pool.wait_ge(s_ident, 2)
            pool.tensor_copy(ident16[:, :], ident[:, :]).then_inc(s_const, 1)

            def rstd(b, u):
                pool.wait_ge(a_ve, upto(a_ve, b, 1))
                pool.tensor_tensor(rs[:, u, :], ve[:, u, :], half_neg[:, 0, :], ALU.pow).then_inc(a_rs, 1)

            def mask(b, p):
                pool.wait_ge(a_e, upto(a_e, b, p + 1))
                pool.sem_inc(passed_pool, 1)
                diag = prob[:, p % 2, :, 0:2 * P].rearrange("p h (t q) -> p h t q", t=2)
                pool.affine_select(out=diag, in_=diag, compare_op=ALU.is_ge, fill=0.0, base=0,
                                   pattern=[[0, 2], [0, 2], [1, P]], channel_multiplier=-1).then_inc(a_pm, 1)

            def spline_rows(b, j, u, w):
                if w == 0:
                    pool.wait_ge(a_phi, upto(a_phi, b, 16))
                steps = 4 * w
                pool.wait_ge(a_sp4, upto(a_sp4, b, steps))
                pool.sem_inc(passed_pool, 1)
                points = cpw[:, w, bass.ds(j, 1), :].rearrange("p j (m o) -> p (j m) o", o=1)
                pool.tensor_tensor(prod[:, :, :], basis[:, u], points.to_broadcast([P, WIN, P]),
                                   ALU.mult).then_inc(a_sp4, 1)
                pool.wait_ge(a_sp4, upto(a_sp4, b, steps + 1))
                pool.tensor_tensor(prod[:, 0:3], prod[:, 0:3], prod[:, 3:6], ALU.add).then_inc(a_sp4, 1)
                pool.wait_ge(a_sp4, upto(a_sp4, b, steps + 2))
                pool.tensor_tensor(prod[:, 0], prod[:, 0], prod[:, 1], ALU.add).then_inc(a_sp4, 1)
                pool.wait_ge(a_sp4, upto(a_sp4, b, steps + 3))
                pool.sem_inc(passed_pool, 1)
                pool.tensor_tensor(spline[:, bass.ds(MT * w + j, 1), P * u:P * u + P], prod[:, 0:1],
                                   prod[:, 2:3], ALU.add).then_inc(a_sp4, 1)

            rstd(0, 0)
            rstd(1, 1)
            rstd(2, 0)
            pool.wait_ge(s_cp, 96)
            pool.wait_ge(s_prep_lo, 7)

            def period(b, j, u, prev=True, nxt=True, nxt2=True, nxt3=True):
                for p in range(NP):
                    mask(b, p)
                    if p == 4 and nxt3:
                        rstd(b + 3, 1 - u)
                    if p in (1, 3, 6):
                        spline_rows(b, j, u, p // 2 if p < 6 else 2)

            run_periods(pool, period)

            def ffn(f):
                def rstd4(g):
                    pool.wait_ge(f.ve, upto(f.ve, g, 1))
                    pool.tensor_tensor(rs[:, :, :], ve[:, :, :], half_neg[:, :, :], ALU.pow).then_inc(f.rs, 1)

                rstd4(0)
                with pool.Fori(1, PAIRS) as g:
                    rstd4(g)

            def g_rstd(n, u):
                pool.wait_ge(g_.ve, upto(g_.ve, n, 1))
                pool.tensor_tensor(rs[:, u, :], ve[:, u, :], half_neg[:, 0, :], ALU.pow).then_inc(g_.rs, 1)

            def g_low_x(n, u):
                pool.wait_ge(g_.gh, upto(g_.gh, n, 1))
                pool.tensor_tensor(gx_lo[:, u], gx, gx_hi[:, u].bitcast(F32), ALU.subtract).then_inc(g_.gl, 1)

            def g_windows(n):
                pool.wait_ge(g_.sg, upto(g_.sg, n, 1))
                pool.wait_ge(g_.qs, upto(g_.qs, n - 1, 1))
                pool.tensor_tensor(qsig, sig[:, 0], win[:, 4], ALU.mult).then_inc(g_.w, 1)
                pool.wait_ge(g_.de, upto(g_.de, n, 1))
                pool.wait_ge(g_.sf, upto(g_.sf, n - 1, 1))
                pool.tensor_tensor(dq, dec, win[:, 0], ALU.mult).then_inc(g_.w, 1)
                pool.wait_ge(g_.sb, upto(g_.sb, n - 1, 1))
                pool.tensor_tensor(dk[:, 0:S - 1], dec[:, 1:S], win[:, 2, 0:S - 1], ALU.mult).then_inc(g_.w, 1)
                pool.wait_ge(g_.kd, upto(g_.kd, n - 1, 1))
                pool.tensor_tensor(kwn, sig[:, 1], win[:, 5], ALU.mult).then_inc(g_.w, 1)

            def g_rr(n):
                pool.wait_ge(g_.vs, upto(g_.vs, n, 1))
                pool.wait_ge(g_.rm, upto(g_.rm, n - 1, 2))
                pool.tensor_tensor(rr[:, :], vs[:, :], half_neg[:, 0, :], ALU.pow).then_inc(g_.rr, 1)

            def g_residual(n):
                pool.wait_ge(g_.rm, upto(g_.rm, n, 2))
                pool.tensor_tensor(rms, rms, gw_row[:, :].rearrange("p (o c) -> p o c", o=1).to_broadcast([P, TB, D]),
                                   ALU.mult).then_inc(g_.mu, 1)
                pool.wait_ge(g_.mu, upto(g_.mu, n, 1))
                pool.wait_ge(g_.gm, upto(g_.gm, n, 1))
                pool.tensor_tensor(rms, rms, gmul, ALU.mult).then_inc(g_.mu, 1)
                pool.wait_ge(g_.mu, upto(g_.mu, n, 2))
                pool.sem_inc(passed_pool, 1)
                tok = X[:, bass.ds(TB * n, TB), :]
                pool.tensor_tensor(tok, tok, rms, ALU.add).then_inc(g_.res, 1)

            def gla():
                g_rstd(0, 0)
                g_low_x(0, 0)
                g_rstd(1, 1)
                pool.wait_ge(s_gload, 32)
                g_windows(0)

                def period(n, u, prev=True, cur=True, nxt=True, nxt2=True):
                    if prev:
                        g_rr(n - 1)
                    if nxt2:
                        g_rstd(n + 2, u)
                    if nxt:
                        g_low_x(n + 1, 1 - u)
                        g_windows(n + 1)
                    if prev:
                        g_residual(n - 1)

                run_gla(pool, period)

            pool.wait_ge(s_fturn, 1)
            pool.memset(causal01[:, :, :], 1.0).then_inc(s_gc, 1)
            pool.wait_ge(s_gc, 1)
            pool.affine_select(out=causal01[:, 0, 0:P], in_=causal01[:, 0, 0:P], compare_op=ALU.is_ge, fill=0.0,
                               base=0, pattern=[[1, P]], channel_multiplier=-1).then_inc(s_gc, 1)
            pool.affine_select(out=causal01[:, 1, :], in_=causal01[:, 1, :], compare_op=ALU.is_ge, fill=0.0,
                               base=-P, pattern=[[1, S]], channel_multiplier=-1).then_inc(s_gc, 1)
            pool.wait_ge(s_flo, 3 * MT // 2)
            pool.memset(dk[:, S - 1:S], 0.0).then_inc(s_gc, 1)
            ffn(f1)
            gla()
            ffn(f2)

        @block.tensor
        def _(pe):
            lead(pe, by_pe + f1.pe + f2.pe + g_.pe)
            pe.wait_ge(s_ident, 2)
            pe.wait_ge(s_w, 16 * 8)
            for n in range(6):
                dst = prep_bank[n][:, :].rearrange("p (c o) -> p c o", c=CT)
                for o in range(CT):
                    for c in range(CT):
                        t = pe.transpose(dst[:, c, P * o:P * o + P], wnat[:, n, o, P * c:P * c + P], ident[:, :])
                t.then_inc(s_prep_ps, 1)
            for n in range(2):
                for c in range(CT):
                    t = pe.transpose(prep_bank[6][:, KG * (2 * n + c):KG * (2 * n + c) + KG],
                                     bnat[:, n, P * c:P * c + P], ident[0:KG, 0:KG])
            t.then_inc(s_prep_ps, 1)
            pe.wait_ge(s_prep_lo, 7)
            pe.wait_ge(s_const, 9)

            def turn_x(b, u):
                pe.wait_ge(a_xn, upto(a_xn, b, 2))
                for c in range(CT):
                    for t in range(TB):
                        i = pe.transpose(bank_t[:, S * c + P * t:S * c + P * t + P], xn[:, t, P * c:P * c + P], ident[:, :])
                i.then_inc(a_xT, 1)

            def proj_qk(b, u, h):
                for n, w in enumerate((wq, wk)):
                    for c in range(CT):
                        cols = slice(P * h, P * h + P)
                        i = mm3(pe, bank_p[:, S * n:S * n + S], w[0][:, c, cols], w[1][:, c, cols],
                                xT_hi[:, u, c, :], xT_lo[:, u, c, :], c == 0, c == CT - 1)
                i.then_inc(a_qkp, 1)

            def proj_v(b, u):
                for t in range(TB):
                    for c in range(CT):
                        tok = slice(P * t, P * t + P)
                        i = mm3(pe, bank_y[:, D * t:D * t + D], xT_hi[:, u, c, tok], xT_lo[:, u, c, tok],
                                wv[0][:, c, :], wv[1][:, c, :], c == 0, c == CT - 1)
                i.then_inc(a_vp, 1)

            def scores(b, u, p):
                h = p // 4
                if p % 4 == 0:
                    pe.wait_ge(a_stk[h], upto(a_stk[h], b, 16 * N_STACK))
                pe.wait_ge(a_mx, upto(a_mx, b, p))
                for n in range(2):
                    hd = (2 * p + n) % HH
                    for t, at_col in ((1, 0), (0, S)):
                        pe.matmul(pair_b[:, n, at_col:at_col + S], stack[0:K_S, u, h, 0, hd, P * t:P * t + P],
                                  stack[0:K_S, u, h, 1, hd, :], start=(t == 1), stop=False)
                    i = pe.matmul(pair_b[:, n, P:3 * P], ident16[:, :],
                                  causal_neg[:, :, :].rearrange("p a b -> p (a b)"), start=False, stop=True)
                i.then_inc(a_sp, 1)

            def turn_max(b, h):
                pe.wait_ge(a_m, upto(a_m, b, 2 * h + 2))
                for t in range(TB):
                    i = pe.transpose(bank_t[0:HH, P * t:P * t + P], mx2[:, h, t, :], ident[:, :])
                i.then_inc(a_mT, 1)

            def shifted(b, u, p):
                h = p // 4
                if p % 4 == 0:
                    pe.wait_ge(a_md[h], upto(a_md[h], b, 32))
                pe.wait_ge(a_e, upto(a_e, b, p))
                for n in range(2):
                    hd = (2 * p + n) % HH
                    for t, at_col in ((1, 0), (0, S)):
                        i = pe.matmul(pair_a[:, n, at_col:at_col + S], stack[0:K_ST, u, h, 1, hd, P * t:P * t + P],
                                      stack[0:K_ST, u, h, 0, hd, :], start=True, stop=True)
                i.then_inc(a_stp, 1)

            def weigh(b, u, p):
                pe.wait_ge(a_pm, upto(a_pm, b, p + 1))
                if p == 0:
                    pe.wait_ge(a_v, upto(a_v, b, 1))
                if p % 4 == 0:
                    pe.wait_ge(a_o, upto(a_o, b, p // 4))
                g = (p % 4) // 2
                for n in range(2):
                    at = 32 * ((2 * p + n) % 4)
                    pe.matmul(bank_o[at:at + 32, S * g:S * g + S], V[:, u, 0, 2 * p + n, :],
                              prob[:, p % 2, n, P:3 * P], start=True, stop=False, tile_position=(0, at))
                for n in range(2):
                    at = 32 * ((2 * p + n) % 4)
                    i = pe.matmul(bank_o[at:at + 32, S * g + P:S * g + S], V[:, u, 1, 2 * p + n, :],
                                  prob[:, p % 2, n, 0:P], start=False, stop=True, tile_position=(0, at))
                i.then_inc(a_pv, 1)

            def turn_o(b, h):
                pe.wait_ge(a_o, upto(a_o, b, h + 1))
                for t in range(TB):
                    for g in range(2):
                        i = pe.transpose(bank_y[:, S * t + P * g:S * t + P * g + P], oT[:, h, g, P * t:P * t + P],
                                         ident[:, :])
                i.then_inc(a_ot, 1)

            def turn_att(b):
                pe.wait_ge(a_at, upto(a_at, b, 2))
                for c in range(CT):
                    for t in range(TB):
                        i = pe.transpose(bank_t[:, S * c + P * t:S * c + P * t + P], att[:, t, P * c:P * c + P], ident[:, :])
                i.then_inc(a_atT, 1)

            def proj_out(b):
                pe.wait_ge(a_atl, upto(a_atl, b, 1))
                for t in range(TB):
                    for c in range(CT):
                        tok = slice(P * t, P * t + P)
                        i = mm3(pe, bank_p[:, D * t:D * t + D], attT_hi[:, c, tok], attT_lo[:, c, tok],
                                wo[0][:, c, :], wo[1][:, c, :], c == 0, c == CT - 1)
                i.then_inc(a_y, 1)

            for b in range(2):
                if b:
                    pe.wait_ge(a_xl, upto(a_xl, b - 1, 1))
                turn_x(b, b)
                pe.wait_ge(a_xl, upto(a_xl, b, 1))
                if b:
                    pe.wait_ge(a_qkl, upto(a_qkl, b - 1, 2))
                proj_qk(b, b, 0)
                pe.wait_ge(a_qkl, upto(a_qkl, b, 1))
                proj_qk(b, b, 1)
                if b == 0:
                    proj_v(0, 0)
            for p in range(4):
                scores(0, 0, p)
            turn_max(0, 0)
            for p in range(4, NP):
                scores(0, 0, p)

            def period(b, j, u, prev=True, nxt=True, nxt2=True, nxt3=True):
                for p in range(NP):
                    shifted(b, u, p)
                    if p or prev:
                        weigh(b if p else b - 1, u if p else 1 - u, (p - 1) % NP)
                    if p == 0 and nxt2:
                        pe.wait_ge(a_ml, upto(a_ml, b, 1))
                        turn_x(b + 2, u)
                    if p == 1:
                        if nxt2:
                            pe.wait_ge(a_xl, upto(a_xl, b + 2, 1))
                        else:
                            pe.wait_ge(a_ml, upto(a_ml, b, 1))
                        turn_max(b, 1)
                    if p == 2 and prev:
                        pe.wait_ge(a_at, upto(a_at, b - 1, 1))
                        turn_o(b - 1, 1)
                    if p == 3:
                        if prev:
                            pe.wait_ge(a_ml, upto(a_ml, b, 2))
                            turn_att(b - 1)
                        if nxt2:
                            pe.wait_ge(a_xl, upto(a_xl, b + 2, 1))
                            pe.wait_ge(a_res, upto(a_res, b - 2, 1))
                            pe.wait_ge(a_qkl, upto(a_qkl, b + 1, 2))
                            proj_qk(b + 2, u, 0)
                    if p == 4 and nxt:
                        pe.wait_ge(a_at, upto(a_at, b - 1, 2))
                        if not prev:
                            pe.wait_ge(a_v, upto(a_v, 0, 1))
                        proj_v(b + 1, 1 - u)
                    if p == 5:
                        if nxt2:
                            pe.wait_ge(a_qkl, upto(a_qkl, b + 2, 1))
                            proj_qk(b + 2, u, 1)
                        if nxt:
                            pe.wait_ge(a_ml, upto(a_ml, b, 2))
                            pe.wait_ge(a_atl, upto(a_atl, b - 1, 1))
                            turn_max(b + 1, 0)
                    if p == 6:
                        if nxt:
                            pe.wait_ge(a_v, upto(a_v, b + 1, 1))
                        else:
                            pe.wait_ge(a_at, upto(a_at, b - 1, 2))
                        turn_o(b, 0)
                    if p == 7 and prev:
                        if nxt2:
                            pe.wait_ge(a_qkl, upto(a_qkl, b + 2, 2))
                        pe.wait_ge(a_res, upto(a_res, b - 2, 1))
                        proj_out(b - 1)
                    if nxt:
                        scores(b + 1, 1 - u, p)

            run_periods(pe, period)
            weigh(B - 1, 1, NP - 1)
            pe.wait_ge(a_at, upto(a_at, B - 1, 1))
            turn_o(B - 1, 1)
            turn_att(B - 1)
            pe.wait_ge(a_res, upto(a_res, B - 2, 1))
            proj_out(B - 1)

            def turn_spline():
                pe.wait_ge(a_sp4, upto(a_sp4, B - 1, 12))
                for n in range(3 * MT // 2):
                    if n == 1:
                        pe.wait_ge(a_res, upto(a_res, B - 1, 1))
                    if n >= 8:
                        pe.wait_ge(s_flo, n - 7)
                    for c in range(CT):
                        for r in range(2):
                            i = pe.transpose(prep_bank[n % 8][:, 2 * P * c + P * r:2 * P * c + P * r + P],
                                             spline[:, 2 * n + r, P * c:P * c + P], ident[:, :])
                    i.then_inc(s_fturn, 1)

            def ffn(f):
                def turn_in(g, h):
                    pe.wait_ge(f.xn, upto(f.xn, g, 4))
                    pe.wait_ge(f.xl, upto(f.xl, g, h))
                    for c in range(CT):
                        for t in range(TB):
                            i = pe.transpose(bank_t[:, S * c + P * t:S * c + P * t + P],
                                             xn_f[:, TB * h + t, P * c:P * c + P], ident[:, :])
                    i.then_inc(f.xT, 1)

                def inner(dst, w_hi, w_lo, u, m):
                    cols = slice(P * m, P * m + P)
                    for c in range(CT):
                        i = mm3(pe, dst, w_hi[:, c, cols], w_lo[:, c, cols], fT_hi[:, u, c, :], fT_lo[:, u, c, :],
                                c == 0, c == CT - 1)
                    return i

                def down(g, m):
                    pe.wait_ge(f.il, upto(f.il, g, m + 1))
                    if m == 0:
                        pe.wait_ge(f.yc, upto(f.yc, g - 1, 2))
                    for h, dst in enumerate((bank_o, bank_y)):
                        rows = slice(P * h, P * h + P)
                        i = mm3(pe, dst[:, :], wd_hi[:, m, rows], wd_lo[:, m, rows], in_hi[:, m % 2, :],
                                in_lo[:, m % 2, :], m == 0, m == MT - 1)
                    i.then_inc(f.dp, 1)

                def turn_out(g, h):
                    pe.wait_ge(f.yc, upto(f.yc, g, 2))
                    pe.wait_ge(f.res, upto(f.res, g, h))
                    for t in range(TB):
                        for c in range(CT):
                            tok = slice(S * h + P * t, S * h + P * t + P)
                            i = pe.transpose(bank_p[:, D * t + P * c:D * t + P * c + P], yT[:, c, tok], ident[:, :])
                    i.then_inc(f.yT, 1)

                def period(g, u, prev=True, nxt=True):
                    pe.wait_ge(f.xl, upto(f.xl, g, 2))
                    for m in range(MT):
                        pe.wait_ge(f.si, upto(f.si, g, m - 1))
                        inner(pair_a[:, m % 2, :], wg_hi, wg_lo, u, m).then_inc(f.gp, 1)
                        pe.wait_ge(f.up, upto(f.up, g, m - 1))
                        inner(pair_b[:, m % 2, :], wu_hi, wu_lo, u, m).then_inc(f.upp, 1)
                        if m or prev:
                            down(g if m else g - 1, (m - 1) % MT)
                        if m in (2, 3) and prev:
                            turn_out(g - 1, m - 2)
                        if m in (4, 5) and nxt:
                            turn_in(g + 1, m - 4)

                turn_in(0, 0)
                turn_in(0, 1)
                run_pairs(period)(pe)
                down(PAIRS - 1, MT - 1)
                turn_out(PAIRS - 1, 0)
                turn_out(PAIRS - 1, 1)

            def g_turn(n):
                pe.wait_ge(g_.xn, upto(g_.xn, n, 2))
                pe.wait_ge(g_.xl, upto(g_.xl, n - 1, 1))
                for c in range(CT):
                    for t in range(TB):
                        i = pe.transpose(bank_t[:, S * c + P * t:S * c + P * t + P], gx[:, t, P * c:P * c + P],
                                         ident[:, :])
                i.then_inc(g_.xT, 1)

            def g_project(n, u):
                pe.wait_ge(g_.xl, upto(g_.xl, n, 1))
                pe.wait_ge(g_.qs, upto(g_.qs, n - 1, 1))
                pe.wait_ge(g_.sg, upto(g_.sg, n - 1, 1))
                for w in range(2):
                    for c in range(CT):
                        i = mm3(pe, bank_p[0:GR, S * w:S * w + S], wqk_hi[:, w, c, :], wqk_lo[:, w, c, :],
                                gT_hi[:, u, c, :], gT_lo[:, u, c, :], c == 0, c == CT - 1)
                i.then_inc(g_.qk, 1)

            def g_products(n):
                pe.wait_ge(g_.qkl, upto(g_.qkl, n, 1))
                pe.wait_ge(g_.am, upto(g_.am, n - 1, 1))
                for t in range(TB):
                    keys = slice(P * t, P * t + P)
                    i = mm3(pe, pair_a[:, 0, S * t:S * t + S], qk_hi[:, 1, keys], qk_lo[:, 1, keys],
                            qk_hi[:, 0, :], qk_lo[:, 0, :], True, True)
                i.then_inc(g_.ap, 1)

            def g_gate(n, u, part):
                if part == 0:
                    pe.wait_ge(g_.xl, upto(g_.xl, n, 1))
                    pe.wait_ge(g_.gm, upto(g_.gm, n - 1, 1))
                else:
                    pe.wait_ge(g_.gol, upto(g_.gol, n, 1))
                for t in range(TB):
                    for c in range(CT):
                        tok = slice(P * t, P * t + P)
                        dst = pair_b[:, 1, D * t:D * t + D]
                        if part == 0:
                            i = mm3(pe, dst, gT_hi[:, u, c, tok], gT_lo[:, u, c, tok], wig[0][:, c, :],
                                    wig[1][:, c, :], t == 0 and c == 0, False)
                        else:
                            i = mm3(pe, dst, goT_hi[:, c, tok], goT_lo[:, c, tok], wog[0][:, c, :],
                                    wog[1][:, c, :], False, t == TB - 1 and c == CT - 1)
                i.then_inc(g_.go if part else g_.go1, 1)

            def g_output(n, u):
                pe.wait_ge(g_.aml, upto(g_.aml, n, 1))
                pe.wait_ge(g_.gl, upto(g_.gl, n, 1))
                pe.wait_ge(g_.gol, upto(g_.gol, n - 1, 1))
                for c in range(CT):
                    chans = slice(P * c, P * c + P)
                    for t in range(TB):
                        i = mm3(pe, pair_a[:, 1, S * c:S * c + S], gx_hi[:, u, t, chans], gx_lo[:, u, t, chans],
                                am_hi[:, t, :], am_lo[:, t, :], t == 0, t == TB - 1)
                i.then_inc(g_.oT, 1)
                pe.wait_ge(g_.rm, upto(g_.rm, n - 1, 2))
                for q in range(TB):
                    for t in range(q + 1):
                        tok = slice(P * q, P * q + P)
                        i = mm3(pe, pair_b[:, 0, D * q:D * q + D], am_hi[:, t, tok], am_lo[:, t, tok],
                                gx_hi[:, u, t, :], gx_lo[:, u, t, :], t == 0, t == q)
                i.then_inc(g_.ot, 1)

            def gla():
                g_turn(0)
                g_project(0, 0)

                def period(n, u, prev=True, cur=True, nxt=True, nxt2=True):
                    if prev:
                        g_gate(n - 1, 1 - u, 0)
                    if nxt:
                        g_turn(n + 1)
                    if prev:
                        g_output(n - 1, 1 - u)
                    if nxt:
                        g_project(n + 1, 1 - u)
                    if prev:
                        g_gate(n - 1, 1 - u, 1)
                    if cur:
                        g_products(n)

                run_gla(pe, period)

            turn_spline()
            pe.wait_ge(s_flo, 3 * MT // 2)
            ffn(f1)
            pe.wait_ge(f1.res, upto(f1.res, PAIRS - 1, 2))
            gla()
            ffn(f2)

        @block.scalar
        def _(act):
            lead(act, by_act + f1.act + f2.act + g_.act)

            def prep_dst(n, part):
                return (wq, wk, wv, wo, wog, wig)[n][part][:, :, :]

            for n in range(6):
                act.wait_ge(s_prep_ps, n + 1)
                act.activation(prep_dst(n, 0), prep_bank[n][:, :].rearrange("p (c o) -> p c o", c=CT),
                               ACT.Copy).then_inc(s_prep_hi, 1)
            act.wait_ge(s_prep_ps, 7)
            turned = prep_bank[6][:, 0:4 * KG].rearrange("p (m k) -> p m k", k=KG)
            for g in range(NG):
                act.activation(wqk_hi[:, :, :, KG * g:KG * g + KG].rearrange("p n c k -> p (n c) k"), turned,
                               ACT.Copy).then_inc(s_prep_hi, 1)

            def copy_xT(b, u, used=True):
                act.wait_ge(a_xT, upto(a_xT, b, 1))
                if used:
                    act.wait_ge(a_vp, upto(a_vp, b - 2, 1))
                act.activation(xT_hi[:, u], bank_t[:, :].rearrange("p (c t) -> p c t", c=CT),
                               ACT.Copy).then_inc(a_xh, 1)

            def copy_qk(b, h, used=True):
                act.wait_ge(a_qkp, upto(a_qkp, b, h + 1))
                if used:
                    act.wait_ge(a_stk[h], upto(a_stk[h], b - 1, 16 * N_STACK))
                act.activation(stage[:, h, 0:4:3, :], bank_p[:, :].rearrange("p (n t) -> p n t", n=2),
                               ACT.Copy).then_inc(a_qkh, 1)

            def copy_v(b, u):
                act.wait_ge(a_vp, upto(a_vp, b, 1))
                act.wait_ge(a_pv, upto(a_pv, b - 2, NP))
                act.activation(V[:, u, :, :, 0:DK], bank_y[:, :].rearrange("p (t h w) -> p t h w", t=TB, h=H),
                               ACT.Copy).then_inc(a_v, 1)

            def exps(b, p):
                act.wait_ge(a_stp, upto(a_stp, b, p + 1))
                act.wait_ge(a_pv, upto(a_pv, b, p - 1))
                act.activation(prob[:, p % 2], pair_a[:, :, P:4 * P], ACT.Exp,
                               scale=DK ** -0.5).then_inc(a_e, 1)

            def copy_o(b, h):
                act.wait_ge(a_pv, upto(a_pv, b, 4 * h + 4))
                act.wait_ge(a_ot, upto(a_ot, b - 1, h + 1))
                act.activation(oT[:, h], bank_o[:, :].rearrange("p (g t) -> p g t", g=2),
                               ACT.Copy).then_inc(a_o, 1)

            def copy_att(b):
                act.wait_ge(a_atT, upto(a_atT, b, 1))
                act.wait_ge(a_y, upto(a_y, b - 1, 1))
                act.activation(attT_hi[:, :, :], bank_t[:, :].rearrange("p (c t) -> p c t", c=CT),
                               ACT.Copy).then_inc(a_ath, 1)

            act.wait_ge(s_const, 7)
            for b in range(2):
                copy_xT(b, b, False)
                copy_qk(b, 0, b > 0)
                copy_qk(b, 1, b > 0)
                if b == 0:
                    copy_v(0, 0)

            def period(b, j, u, prev=True, nxt=True, nxt2=True, nxt3=True):
                for p in range(NP):
                    exps(b, p)
                    if p == 0:
                        if prev:
                            copy_o(b - 1, 1)
                        if nxt2:
                            copy_xT(b + 2, u)
                    if p == 3:
                        if prev:
                            copy_att(b - 1)
                        if nxt2:
                            copy_qk(b + 2, 0)
                    if p == 4:
                        copy_o(b, 0)
                        if nxt:
                            copy_v(b + 1, 1 - u)
                    if p == 5 and nxt2:
                        copy_qk(b + 2, 1)

            run_periods(act, period)
            copy_o(B - 1, 1)
            copy_att(B - 1)

            def split_spline():
                for n in range(3 * MT // 2):
                    act.wait_ge(s_fturn, n + 1)
                    src = prep_bank[n % 8][:, :]
                    if n < MT:
                        dst = (wg_hi, wu_hi)[n // 4][:, :, 2 * P * (n % 4):2 * P * (n % 4) + 2 * P]
                        act.activation(dst, src.rearrange("p (c o) -> p c o", c=CT), ACT.Copy).then_inc(s_fhi, 1)
                    else:
                        cols = slice(64 * (n - MT), 64 * (n - MT) + 64)
                        for c in range(CT):
                            i = act.activation(wd_hi[:, c::CT, cols], turned_down(src)[:, c], ACT.Copy)
                        i.then_inc(s_fhi, 1)

            def ffn(f):
                def high_in(g, u, h):
                    act.wait_ge(f.xT, upto(f.xT, g, h + 1))
                    act.wait_ge(f.upp, upto(f.upp, g - 2, MT))
                    act.activation(fT_hi[:, u, :, S * h:S * h + S], bank_t[:, :].rearrange("p (c t) -> p c t", c=CT),
                                   ACT.Copy).then_inc(f.xh, 1)

                def silu(g, m):
                    act.wait_ge(f.gp, upto(f.gp, g, m + 1))
                    act.wait_ge(f.up, upto(f.up, g, m - 1))
                    act.activation(gact[:, m % 2, :], pair_a[:, m % 2, :], ACT.Silu).then_inc(f.si, 1)

                def high_inner(g, m):
                    act.wait_ge(f.up, upto(f.up, g, m + 1))
                    act.wait_ge(f.dp, upto(f.dp, g, m - 1))
                    act.activation(in_hi[:, m % 2, :], inter[:, m % 2, :], ACT.Copy).then_inc(f.ih, 1)

                def copy_y(g):
                    act.wait_ge(f.dp, upto(f.dp, g, MT))
                    act.wait_ge(f.yT, upto(f.yT, g - 1, 2))
                    for c, src in enumerate((bank_o, bank_y)):
                        act.activation(yT[:, c, :], src[:, :], ACT.Copy).then_inc(f.yc, 1)

                def period(g, u, prev=True, nxt=True):
                    for m in range(MT):
                        silu(g, m)
                        high_inner(g, m)
                        if m == 0 and prev:
                            copy_y(g - 1)
                        if m in (4, 5) and nxt:
                            high_in(g + 1, 1 - u, m - 4)

                high_in(0, 0, 0)
                high_in(0, 0, 1)
                run_pairs(period)(act)
                copy_y(PAIRS - 1)

            def g_high_turned(n, u):
                act.wait_ge(g_.xT, upto(g_.xT, n, 1))
                act.wait_ge(g_.go1, upto(g_.go1, n - 2, 1))
                act.activation(gT_hi[:, u], bank_t[:, :].rearrange("p (c t) -> p c t", c=CT),
                               ACT.Copy).then_inc(g_.xh, 1)

            def g_high_x(n, u):
                act.wait_ge(g_.xn, upto(g_.xn, n, 2))
                act.wait_ge(g_.ot, upto(g_.ot, n - 2, 1))
                act.activation(gx_hi[:, u], gx, ACT.Copy).then_inc(g_.gh, 1)

            def g_sigmoids(n):
                act.wait_ge(g_.qk, upto(g_.qk, n, 1))
                act.wait_ge(g_.w, upto(g_.w, n - 1, 4))
                act.activation(sig, bank_p[0:GR, :].rearrange("p (w t) -> p w t", w=2), ACT.Sigmoid).then_inc(g_.sg, 1)
                act.wait_ge(g_.sg, upto(g_.sg, n, 1))
                act.activation(dec, sig[:, 1], ACT.Sigmoid, scale=-1.0).then_inc(g_.de, 1)

            def g_high_qk(n):
                act.wait_ge(g_.kd, upto(g_.kd, n, 1))
                act.wait_ge(g_.ap, upto(g_.ap, n - 1, 1))
                act.activation(qk_hi[:, :, :], qk, ACT.Copy).then_inc(g_.qkh, 1)

            def g_high_am(n):
                act.wait_ge(g_.am, upto(g_.am, n, 1))
                act.wait_ge(g_.ot, upto(g_.ot, n - 1, 1))
                act.activation(am_hi[:, :, :], am, ACT.Copy).then_inc(g_.amh, 1)

            def g_high_out(n):
                act.wait_ge(g_.oT, upto(g_.oT, n, 1))
                act.wait_ge(g_.go, upto(g_.go, n - 1, 1))
                act.activation(goT_hi[:, :, :], pair_a[:, 1, :].rearrange("p (c t) -> p c t", c=CT),
                               ACT.Copy).then_inc(g_.goh, 1)

            def g_squares(n):
                act.wait_ge(g_.ot, upto(g_.ot, n, 1))
                act.wait_ge(g_.vs, upto(g_.vs, n - 1, 1))
                for t in range(TB):
                    if t:
                        act.wait_ge(g_.sq, upto(g_.sq, n, 1))
                    else:
                        act.wait_ge(g_.sq, upto(g_.sq, n - 1, 2))
                    act.activation(junk[:, :], pair_b[:, 0, D * t:D * t + D], ACT.Square,
                                   accum_out=ssq[:, t:t + 1]).then_inc(g_.sq, 1)

            def g_normalise(n):
                act.wait_ge(g_.rr, upto(g_.rr, n, 1))
                act.wait_ge(g_.res, upto(g_.res, n - 1, 1))
                for t in range(TB):
                    act.activation(rms[:, t, :], pair_b[:, 0, D * t:D * t + D], ACT.Copy,
                                   scale=rr[:, t:t + 1]).then_inc(g_.rm, 1)

            def g_gate_sigmoid(n):
                act.wait_ge(g_.go, upto(g_.go, n, 1))
                act.wait_ge(g_.gm, upto(g_.gm, n - 1, 1))
                act.activation(gsig, pair_b[:, 1, :].rearrange("p (t c) -> p t c", t=TB),
                               ACT.Sigmoid).then_inc(g_.gs, 1)

            def gla():
                g_high_turned(0, 0)
                g_high_x(0, 0)
                g_sigmoids(0)

                def period(n, u, prev=True, cur=True, nxt=True, nxt2=True):
                    if prev:
                        g_high_am(n - 1)
                    if nxt:
                        g_high_turned(n + 1, 1 - u)
                    if prev:
                        g_high_out(n - 1)
                        g_squares(n - 1)
                    if cur:
                        g_high_qk(n)
                    if nxt:
                        g_high_x(n + 1, 1 - u)
                        g_sigmoids(n + 1)
                    if prev:
                        g_normalise(n - 1)
                        g_gate_sigmoid(n - 1)

                run_gla(act, period)

            split_spline()
            ffn(f1)
            gla()
            ffn(f2)

        @block.vector
        def _(dve):
            lead(dve, by_dve + f1.dve + f2.dve + g_.dve)

            def stats(b, u):
                for t in range(TB):
                    dve.bn_stats(st[:, u, t, :], X[:, bass.ds(TB * b + t, 1), :]).then_inc(a_bn, 1)
                dve.wait_ge(a_bn, upto(a_bn, b, TB))
                dve.sem_inc(passed_dve, 1)
                for t in range(TB):
                    dve.bn_aggr(mv[:, u, t, :], st[:, u, t, :]).then_inc(a_mv, 1)
                dve.wait_ge(a_mv, upto(a_mv, b, 2))
                dve.tensor_scalar(ve[:, u, :], mv[:, u, :, 1], EPS, None, ALU.add).then_inc(a_ve, 1)

            def normalise(b, u):
                dve.wait_ge(a_rs, upto(a_rs, b, 1))
                dve.wait_ge(a_xT, upto(a_xT, b - 1, 1))
                for t in range(TB):
                    dve.tensor_scalar(xn[:, t, :], X[:, bass.ds(TB * b + t, 1), :], mv[:, u, t, 0:1],
                                      rs[:, u, t:t + 1], ALU.subtract, ALU.mult).then_inc(a_xn, 1)

            for n in range(6):
                hi, lo = (wq, wk, wv, wo, wog, wig)[n]
                dve.wait_ge(s_prep_hi, n + 1)
                dve.tensor_tensor(lo[:, :, :], prep_bank[n][:, :].rearrange("p (c o) -> p c o", c=CT),
                                  hi[:, :, :].bitcast(F32), ALU.subtract).then_inc(s_prep_lo, 1)
                if n < 2:
                    dve.wait_ge(s_x[n], 16)
                    stats(n, n)
            dve.wait_ge(s_prep_hi, 6 + NG)
            turned = prep_bank[6][:, 0:4 * KG].rearrange("p (m k) -> p m k", k=KG)
            for g in range(NG):
                cols = slice(KG * g, KG * g + KG)
                i = dve.tensor_tensor(wqk_lo[:, :, :, cols].rearrange("p n c k -> p (n c) k"), turned,
                                      wqk_hi[:, :, :, cols].rearrange("p n c k -> p (n c) k").bitcast(F32),
                                      ALU.subtract)
            i.then_inc(s_prep_lo, 1)

            def low_xT(b, u, used=True):
                dve.wait_ge(a_xh, upto(a_xh, b, 1))
                if used:
                    dve.wait_ge(a_vp, upto(a_vp, b - 2, 1))
                dve.tensor_tensor(xT_lo[:, u], bank_t[:, :].rearrange("p (c t) -> p c t", c=CT),
                                  xT_hi[:, u].bitcast(F32), ALU.subtract).then_inc(a_xl, 1)

            def low_qk(b, h):
                dve.wait_ge(a_qkh, upto(a_qkh, b, h + 1))
                dve.tensor_tensor(stage[:, h, 2:0:-1, :], bank_p[:, :].rearrange("p (n t) -> p n t", n=2),
                                  stage[:, h, 0:4:3, :].bitcast(F32), ALU.subtract).then_inc(a_qkl, 1)

            def maxima(b, p):
                dve.wait_ge(a_sp, upto(a_sp, b, p + 1))
                if p % 4 == 0:
                    dve.wait_ge(a_m, upto(a_m, b - 1, 2 * (p // 4) + 2))
                h, hd = p // 4, (2 * p) % HH
                dve.tensor_reduce(mx[:, h, hd:hd + 2, :], pair_b[:, :, 0:3 * P].rearrange("p n (t k) -> p n t k", t=3),
                                  AX.X, ALU.max).then_inc(a_mx, 1)

            def merge_max(b, h):
                dve.wait_ge(a_mx, upto(a_mx, b, 4 * h + 4))
                dve.wait_ge(a_mT, upto(a_mT, b - 1, h + 1))
                dve.tensor_copy(mx2[:, h, 0, :], mx[:, h, :, 2]).then_inc(a_m, 1)
                dve.tensor_tensor(mx2[:, h, 1, :], mx[:, h, :, 0], mx[:, h, :, 1], ALU.max).then_inc(a_m, 1)

            def split_max(b, h):
                dve.wait_ge(a_mT, upto(a_mT, b, h + 1))
                dve.wait_ge(a_md[h], upto(a_md[h], b - 1, 32))
                dve.tensor_scalar(mrow[:, h, 0, :], bank_t[0:HH, 0:S], -1.0, None, ALU.mult).then_inc(a_mh, 1)
                dve.wait_ge(a_mh, upto(a_mh, b, h + 1))
                dve.scalar_tensor_tensor(out=mrow[:, h, 1, :], in0=bank_t[0:HH, 0:S], scalar=-1.0,
                                         in1=mrow[:, h, 0, :].bitcast(F32), op0=ALU.mult,
                                         op1=ALU.subtract).then_inc(a_ml, 1)

            def divide(b, h):
                dve.wait_ge(a_ot, upto(a_ot, b, h + 1))
                dve.wait_ge(a_at, upto(a_at, b - 1, h + 1))
                dve.reciprocal(rden[:, h], bank_y4[:, :, :, DK]).then_inc(a_rd, 1)
                dve.wait_ge(a_rd, upto(a_rd, b, h + 1))
                dve.wait_ge(a_atT, upto(a_atT, b - 1, 1))
                dst = att[:, :, P * h:P * h + P].rearrange("p t (h w) -> p t h w", w=DK)
                dve.tensor_tensor(dst, bank_y4[:, :, :, 0:DK],
                                  rden[:, h].rearrange("p t (h o) -> p t h o", o=1).to_broadcast([P, TB, HH, DK]),
                                  ALU.mult).then_inc(a_at, 1)

            def low_att(b):
                dve.wait_ge(a_ath, upto(a_ath, b, 1))
                dve.wait_ge(a_y, upto(a_y, b - 1, 1))
                dve.tensor_tensor(attT_lo[:, :, :], bank_t[:, :].rearrange("p (c t) -> p c t", c=CT),
                                  attT_hi[:, :, :].bitcast(F32), ALU.subtract).then_inc(a_atl, 1)

            def residual(b):
                dve.wait_ge(a_y, upto(a_y, b, 1))
                tok = X[:, bass.ds(TB * b, TB), :]
                dve.tensor_tensor(tok, bank_p[:, :].rearrange("p (t c) -> p t c", t=TB), tok,
                                  ALU.add).then_inc(a_res, 1)

            normalise(0, 0)
            normalise(1, 1)
            dve.wait_ge(s_x[2], 16)
            for b in range(2):
                low_xT(b, b, False)
                low_qk(b, 0)
                low_qk(b, 1)
            stats(2, 0)
            normalise(2, 0)
            for p in range(4):
                maxima(0, p)
            merge_max(0, 0)
            split_max(0, 0)
            for p in range(4, NP):
                maxima(0, p)
            merge_max(0, 1)

            def period(b, j, u, prev=True, nxt=True, nxt2=True, nxt3=True):
                for p in range(NP):
                    if p == 0 and nxt2:
                        low_xT(b + 2, u)
                    if p == 1:
                        split_max(b, 1)
                    if p == 2 and prev:
                        divide(b - 1, 1)
                    if p == 3:
                        if prev:
                            low_att(b - 1)
                    if p == 4 and nxt3:
                        stats(b + 3, 1 - u)
                    if p == 6:
                        divide(b, 0)
                        if nxt3:
                            normalise(b + 3, 1 - u)
                    if p == 7 and prev:
                        residual(b - 1)
                    if nxt:
                        if p == 5:
                            split_max(b + 1, 0)
                        maxima(b + 1, p)
                        if p == 3:
                            merge_max(b + 1, 0)
                        if p == 7:
                            merge_max(b + 1, 1)
                    if nxt2 and p in (3, 5):
                        low_qk(b + 2, p // 4)

            run_periods(dve, period)
            divide(B - 1, 1)
            low_att(B - 1)
            residual(B - 1)

            def split_spline():
                for n in range(3 * MT // 2):
                    dve.wait_ge(s_fhi, n + 1)
                    src = prep_bank[n % 8][:, :]
                    if n < MT:
                        cols = slice(2 * P * (n % 4), 2 * P * (n % 4) + 2 * P)
                        hi, lo = ((wg_hi, wg_lo), (wu_hi, wu_lo))[n // 4]
                        i = dve.tensor_tensor(lo[:, :, cols], src.rearrange("p (c o) -> p c o", c=CT),
                                              hi[:, :, cols].bitcast(F32), ALU.subtract)
                    else:
                        cols = slice(64 * (n - MT), 64 * (n - MT) + 64)
                        for c in range(CT):
                            i = dve.tensor_tensor(wd_lo[:, c::CT, cols], turned_down(src)[:, c],
                                                  wd_hi[:, c::CT, cols].bitcast(F32), ALU.subtract)
                    i.then_inc(s_flo, 1)

            def ffn(f):
                def stats4(g):
                    for t in range(2 * TB):
                        dve.bn_stats(st[:, t // TB, t % TB, :],
                                     X[:, bass.ds(2 * TB * g + t, 1), :]).then_inc(f.bn, 1)
                    dve.wait_ge(f.bn, upto(f.bn, g, 4))
                    dve.sem_inc(passed_dve, 1)
                    for t in range(2 * TB):
                        dve.bn_aggr(mv[:, t // TB, t % TB, :], st[:, t // TB, t % TB, :]).then_inc(f.mv, 1)
                    dve.wait_ge(f.mv, upto(f.mv, g, 4))
                    dve.tensor_scalar(ve[:, :, :], mv[:, :, :, 1], EPS, None, ALU.add).then_inc(f.ve, 1)

                def normalise4(g, tiles):
                    dve.wait_ge(f.rs, upto(f.rs, g, 1))
                    dve.wait_ge(f.xT, upto(f.xT, g - 1, 2))
                    for t in tiles:
                        dve.tensor_scalar(xn_f[:, t, :], X[:, bass.ds(2 * TB * g + t, 1), :],
                                          mv[:, t // TB, t % TB, 0:1], rs[:, t // TB, t % TB:t % TB + 1],
                                          ALU.subtract, ALU.mult).then_inc(f.xn, 1)

                def low_in(g, u, h):
                    dve.wait_ge(f.xh, upto(f.xh, g, h + 1))
                    dve.wait_ge(f.upp, upto(f.upp, g - 2, MT))
                    dst = slice(S * h, S * h + S)
                    dve.tensor_tensor(fT_lo[:, u, :, dst], bank_t[:, :].rearrange("p (c t) -> p c t", c=CT),
                                      fT_hi[:, u, :, dst].bitcast(F32), ALU.subtract).then_inc(f.xl, 1)

                def gated(g, m):
                    dve.wait_ge(f.upp, upto(f.upp, g, m + 1))
                    dve.wait_ge(f.si, upto(f.si, g, m + 1))
                    dve.wait_ge(f.ih, upto(f.ih, g, m - 1))
                    dve.tensor_tensor(inter[:, m % 2, :], gact[:, m % 2, :], pair_b[:, m % 2, :],
                                      ALU.mult).then_inc(f.up, 1)

                def low_inner(g, m):
                    dve.wait_ge(f.ih, upto(f.ih, g, m + 1))
                    dve.tensor_tensor(in_lo[:, m % 2, :], inter[:, m % 2, :], in_hi[:, m % 2, :].bitcast(F32),
                                      ALU.subtract).then_inc(f.il, 1)

                def residual2(g, h):
                    dve.wait_ge(f.yT, upto(f.yT, g, h + 1))
                    tok = X[:, bass.ds(2 * TB * g + TB * h, TB), :]
                    dve.tensor_tensor(tok, bank_p[:, :].rearrange("p (t c) -> p t c", t=TB), tok,
                                      ALU.add).then_inc(f.res, 1)

                def period(g, u, prev=True, nxt=True):
                    for m in range(MT):
                        gated(g, m)
                        low_inner(g, m)
                        if m == 0 and nxt:
                            stats4(g + 1)
                        if m in (1, 2) and nxt:
                            normalise4(g + 1, range(TB * (m - 1), TB * m))
                        if m in (2, 3) and prev:
                            residual2(g - 1, m - 2)
                        if m in (4, 5) and nxt:
                            low_in(g + 1, 1 - u, m - 4)

                stats4(0)
                normalise4(0, range(2 * TB))
                low_in(0, 0, 0)
                low_in(0, 0, 1)
                run_pairs(period)(dve)
                residual2(PAIRS - 1, 0)
                residual2(PAIRS - 1, 1)

            def g_stats(n, u):
                for t in range(TB):
                    dve.bn_stats(st[:, u, t, :], X[:, bass.ds(TB * n + t, 1), :]).then_inc(g_.bn, 1)
                dve.wait_ge(g_.bn, upto(g_.bn, n, TB))
                dve.sem_inc(passed_dve, 1)
                for t in range(TB):
                    dve.bn_aggr(mv[:, u, t, :], st[:, u, t, :]).then_inc(g_.mv, 1)
                dve.wait_ge(g_.mv, upto(g_.mv, n, TB))
                dve.tensor_scalar(ve[:, u, :], mv[:, u, :, 1], EPS, None, ALU.add).then_inc(g_.ve, 1)

            def g_norm(n, u):
                dve.wait_ge(g_.rs, upto(g_.rs, n, 1))
                dve.wait_ge(g_.xT, upto(g_.xT, n - 1, 1))
                dve.wait_ge(g_.gl, upto(g_.gl, n - 1, 1))
                for t in range(TB):
                    dve.tensor_scalar(gx[:, t, :], X[:, bass.ds(TB * n + t, 1), :], mv[:, u, t, 0:1],
                                      rs[:, u, t:t + 1], ALU.subtract, ALU.mult).then_inc(g_.xn, 1)

            def g_low_turned(n, u):
                dve.wait_ge(g_.xh, upto(g_.xh, n, 1))
                dve.wait_ge(g_.go1, upto(g_.go1, n - 2, 1))
                dve.tensor_tensor(gT_lo[:, u], bank_t[:, :].rearrange("p (c t) -> p c t", c=CT),
                                  gT_hi[:, u].bitcast(F32), ALU.subtract).then_inc(g_.xl, 1)

            def g_silu_q(n):
                dve.wait_ge(g_.w, upto(g_.w, n, 1))
                dve.tensor_tensor(qsil, bank_p[0:GR, 0:S], qsig, ALU.mult).then_inc(g_.qs, 1)

            def g_decays(n):
                dve.wait_ge(g_.w, upto(g_.w, n, 3))
                dve.wait_ge(g_.qd, upto(g_.qd, n - 1, 1))
                dve.tensor_tensor_scan(fq, dq, win[:, 1], 0.0, ALU.mult, ALU.add).then_inc(g_.sf, 1)
                dve.tensor_tensor_scan(fk[64:GR, ::-1], dk[64:GR, ::-1], win[64:GR, 3, ::-1], 0.0, ALU.mult,
                                       ALU.add).then_inc(g_.sb, 1)
                dve.wait_ge(g_.sf, upto(g_.sf, n, 1))
                dve.reciprocal(fk[0:64], fq[0:64]).then_inc(g_.rc, 1)

            def g_decayed(n):
                dve.wait_ge(g_.qs, upto(g_.qs, n, 1))
                dve.wait_ge(g_.qkh, upto(g_.qkh, n - 1, 1))
                dve.tensor_tensor(qk[:, 0], qsil, fq, ALU.mult).then_inc(g_.qd, 1)
                dve.wait_ge(g_.w, upto(g_.w, n, 4))
                dve.wait_ge(g_.rc, upto(g_.rc, n, 1))
                dve.tensor_tensor(qk[:, 1], kwn, fk, ALU.mult).then_inc(g_.kd, 1)

            def g_low_qk(n):
                dve.wait_ge(g_.qkh, upto(g_.qkh, n, 1))
                dve.tensor_tensor(qk_lo[:, :, :], qk, qk_hi[:, :, :].bitcast(F32), ALU.subtract).then_inc(g_.qkl, 1)

            def g_masked(n):
                dve.wait_ge(g_.ap, upto(g_.ap, n, 1))
                dve.wait_ge(g_.amh, upto(g_.amh, n - 1, 1))
                dve.scalar_tensor_tensor(out=am, in0=pair_a[:, 0, :].rearrange("p (k t) -> p k t", k=TB), scalar=BIG,
                                         in1=causal01[:, :, :], op0=ALU.min, op1=ALU.mult).then_inc(g_.am, 1)

            def g_low_am(n):
                dve.wait_ge(g_.amh, upto(g_.amh, n, 1))
                dve.tensor_tensor(am_lo[:, :, :], am, am_hi[:, :, :].bitcast(F32), ALU.subtract).then_inc(g_.aml, 1)

            def g_low_out(n):
                dve.wait_ge(g_.goh, upto(g_.goh, n, 1))
                dve.tensor_tensor(goT_lo[:, :, :], pair_a[:, 1, :].rearrange("p (c t) -> p c t", c=CT),
                                  goT_hi[:, :, :].bitcast(F32), ALU.subtract).then_inc(g_.gol, 1)

            def g_mean_square(n):
                dve.wait_ge(g_.sq, upto(g_.sq, n, 2))
                dve.wait_ge(g_.rr, upto(g_.rr, n - 1, 1))
                dve.tensor_scalar(vs[:, :], ssq[:, :], 1.0 / D, EPS, ALU.mult, ALU.add).then_inc(g_.vs, 1)

            def g_gated(n):
                dve.wait_ge(g_.gs, upto(g_.gs, n, 1))
                dve.wait_ge(g_.mu, upto(g_.mu, n - 1, 2))
                dve.tensor_tensor(gmul, pair_b[:, 1, :].rearrange("p (t c) -> p t c", t=TB), gsig,
                                  ALU.mult).then_inc(g_.gm, 1)

            def gla():
                dve.wait_ge(s_gload, 32)
                dve.wait_ge(s_gc, 4)
                dve.wait_ge(f1.res, upto(f1.res, PAIRS - 1, 2))
                g_stats(0, 0)
                g_norm(0, 0)
                g_stats(1, 1)
                g_low_turned(0, 0)
                g_norm(1, 1)

                def period(n, u, prev=True, cur=True, nxt=True, nxt2=True):
                    if prev:
                        g_masked(n - 1)
                    if cur:
                        g_silu_q(n)
                    if prev:
                        g_low_am(n - 1)
                    if nxt:
                        g_low_turned(n + 1, 1 - u)
                    if nxt2:
                        g_stats(n + 2, u)
                    if cur:
                        g_decays(n)
                    if prev:
                        g_low_out(n - 1)
                    if cur:
                        g_decayed(n)
                    if prev:
                        g_mean_square(n - 1)
                    if cur:
                        g_low_qk(n)
                    if prev:
                        g_gated(n - 1)
                    if nxt2:
                        g_norm(n + 2, u)

                run_gla(dve, period)

            dve.wait_ge(s_fhi, 1)
            split_spline()
            dve.wait_ge(a_res, upto(a_res, B - 1, 1))
            ffn(f1)
            gla()
            dve.wait_ge(g_.res, upto(g_.res, B - 1, 1))
            ffn(f2)


def kernel(**inputs):
    import concourse.bacc as bacc
    from concourse.bass_utils import run_bass_kernel_spmd

    arrays = {}
    for name, value in inputs.items():
        if not name.endswith("_cp"):
            arrays[name.replace("L0_", "in_")] = np.ascontiguousarray(value)
    cps = np.zeros((3, N_CP), np.float32)
    for n, name in enumerate(("gate", "up", "down")):
        cps[n, FRONT:FRONT + N_CTRL] = inputs[f"L0_ffn_{name}_cp"]
    arrays["control_points"] = cps
    arrays["spline_basis"] = spline_basis()
    arrays["decay_windows"] = decay_windows()
    nc = bacc.Bacc("TRN2", target_bir_lowering=False, num_devices=1)
    args = [nc.dram_tensor(n, a.shape, mybir.dt.from_np(a.dtype), kind="ExternalInput").ap()
            for n, a in arrays.items()]
    result = nc.dram_tensor("result", (B, S, D), F32, kind="ExternalOutput").ap()
    build(nc, *args, result)
    return run_bass_kernel_spmd(nc, [arrays], core_ids=[0]).results[0]["result"]
```

```python
from contextlib import ExitStack

import numpy as np

import concourse.bass as bass
from concourse import mybir

ACT = mybir.ActivationFunctionType
ALU = mybir.AluOpType
AX = mybir.AxisListType
F32 = mybir.dt.float32
F32R = mybir.dt.float32r
BF16 = mybir.dt.bfloat16

P = 128
B = 16
S = 256
D = 256
NT = B * S // P
TB = S // P
CT = D // P
H = 16
DK = D // H
HH = 8
NP = H // 2
EPS = 1e-5
NEG = -3.0e38
INTER = 1024
MT = INTER // P
N_CTRL = 2033
WIN = 6
FRONT = 2
BACK = 3
N_CP = FRONT + N_CTRL + BACK
KG = 16
NG = 7
GR = NG * KG
GROW = 2.0 ** 60
BIG = 3.0e38
LEAD = 2

K_S = 65
K_ST = 67
ZROW = 64
MROW = 65


class Signals:
    pass


def spline_basis():
    n = INTER * D
    t = np.linspace(0.0, N_CTRL - 1.0, n, dtype=np.float64)
    i = np.clip(np.floor(t).astype(np.int64), 0, N_CTRL - 2)
    f = (t - i).astype(np.float32).astype(np.float64)
    coef = [
        0.5 * (-f + 2 * f * f - f * f * f),
        0.5 * (2 - 5 * f * f + 3 * f * f * f),
        0.5 * (f + 4 * f * f - 3 * f * f * f),
        0.5 * (-f * f + f * f * f),
    ]
    rows = np.arange(n) // D
    base = 127 * (rows // 64) + 2 * (rows % 64) - FRONT
    phi = np.zeros((n, WIN))
    for k in range(4):
        m = np.clip(i + k - 1, 0, N_CTRL - 1) - base
        assert m.min() >= 0 and m.max() < WIN
        np.add.at(phi, (np.arange(n), m), coef[k])
    phi = phi.reshape(MT, P, D, WIN).transpose(0, 1, 3, 2)
    return np.ascontiguousarray(phi.reshape(MT, P, WIN * D).astype(np.float32))


def decay_windows():
    w = np.zeros((GR, 6, S), np.float32)
    run, start, krun, kstart, qwin, kwin = (w[:, n] for n in range(6))
    for g in range(4):
        r = slice(KG * g, KG * g + KG)
        run[r] = 1.0
        run[r, ::64] = 0.0
        start[r, ::64] = GROW
        qwin[r, 64 * g:64 * g + 64] = 1.0
        kwin[r, 64 * g:64 * g + 64] = KG ** -0.5
    for g, ref, length in ((4, 64, 64), (5, 192, 64), (6, 128, 128)):
        r = slice(KG * g, KG * g + KG)
        run[r, ref + 1:ref + length] = 1.0
        start[r, ref] = 1.0
        krun[r, ref - length:ref] = 1.0
        kstart[r, ref] = 1.0
        qwin[r, ref:ref + length] = 1.0
        kwin[r, ref - length:ref] = KG ** -0.5
    return w


def build(nc, x, a_wq, a_wk, a_wv, a_wo, b_wq, b_wk, b_wog, b_wig, g_weight, cps, phi, windows, out):
    outer = ExitStack()
    with outer:
        def sb(name, shape, dt, where=outer):
            return where.enter_context(nc.sbuf_tensor(name, shape, dt))

        sems = {}

        def sem(name):
            sems[name] = outer.enter_context(nc.semaphore(name))
            return sems[name]

        bank = [outer.enter_context(nc.psum_tensor(f"bank{n}", [P, 512], F32)) for n in range(4)]
        pair_a = outer.enter_context(nc.psum_tensor("pair_a", [P, 2, 512], F32))
        pair_b = outer.enter_context(nc.psum_tensor("pair_b", [P, 2, 512], F32))
        bank_t, bank_p, bank_o, bank_y = bank
        prep_bank = bank + [pair_a[:, 0], pair_a[:, 1], pair_b[:, 0], pair_b[:, 1]]
        fill_bank = prep_bank[2:] + prep_bank[0:2]

        X = sb("X", [P, NT, D], F32)
        ident = sb("ident", [P, P], F32)
        ident16 = sb("ident16", [P, P], BF16)
        causal_neg = sb("causal_neg", [P, 2, P], BF16)
        half_neg = sb("half_neg", [P, 2, TB], F32)
        wog = sb("wog_hi", [P, CT, D], F32R), sb("wog_lo", [P, CT, D], F32R)
        wig = sb("wig_hi", [P, CT, D], F32R), sb("wig_lo", [P, CT, D], F32R)
        wqk_hi = sb("wqk_hi", [P, 2, CT, GR], F32R)
        wqk_lo = sb("wqk_lo", [P, 2, CT, GR], F32R)
        st = sb("st", [P, 2, TB, 6], F32)
        mv = sb("mv", [P, 2, TB, 2], F32)
        ve = sb("ve", [P, 2, TB], F32)
        rs = sb("rs", [P, 2, TB], F32)
        negm = sb("negm", [P, 2, TB], F32)
        nmr = sb("nmr", [P, 2, TB], F32)
        quarter = sb("quarter", [P, 1], F32)
        spline = sb("spline", [P, 3 * MT, D], F32)
        wnat = spline[:, 0:6 * CT, :].rearrange("p (w o) c -> p w o c", w=6)
        bnat = spline[0:KG, 6 * CT:6 * CT + 2, :]

        with ExitStack() as at:
            wq, wk, wv, wo = ((sb(n + "_hi", [P, CT, D], F32R, at), sb(n + "_lo", [P, CT, D], F32R, at))
                              for n in ("wq", "wk", "wv", "wo"))
            cpw = sb("cpw", [P, 3, MT, WIN], F32, at)
            basis = sb("basis", [P, 2, WIN, P], F32, at)
            prod = sb("prod", [P, WIN, P], F32, at)
            xn = sb("xn", [P, TB, D], F32, at)
            xT_hi = sb("xT_hi", [P, 2, CT, S], F32R, at)
            xT_lo = sb("xT_lo", [P, 2, CT, S], F32R, at)
            stage = sb("stage", [P, 2, 4, S], F32R, at)
            stack = sb("stack", [K_ST, 2, 2, 2, HH, S], F32R, at)
            V = sb("V", [P, 2, TB, H, 32], F32, at)
            mx = sb("mx", [P, 2, HH, 3], F32, at)
            mx2 = sb("mx2", [P, 2, TB, HH], F32, at)
            mrow = sb("mrow", [HH, 2, 2, S], F32R, at)
            prob = sb("prob", [P, 2, 2, 3 * P], F32, at)
            oT = sb("oT", [P, 2, 2, S], F32, at)
            rden = sb("rden", [P, 2, TB, HH], F32, at)
            att = sb("att", [P, TB, D], F32, at)
            attT_hi = sb("attT_hi", [P, CT, S], F32R, at)
            attT_lo = sb("attT_lo", [P, CT, S], F32R, at)

        with ExitStack() as ft:
            wg_hi = sb("wg_hi", [P, CT, INTER], F32R, ft)
            wg_lo = sb("wg_lo", [P, CT, INTER], F32R, ft)
            wu_hi = sb("wu_hi", [P, CT, INTER], F32R, ft)
            wu_lo = sb("wu_lo", [P, CT, INTER], F32R, ft)
            wd_hi = sb("wd_hi", [P, MT, D], F32R, ft)
            wd_lo = sb("wd_lo", [P, MT, D], F32R, ft)
            xn_f = sb("xn_f", [P, 2 * TB, D], F32, ft)
            fT_hi = sb("fT_hi", [P, 2, CT, 2 * S], F32R, ft)
            fT_lo = sb("fT_lo", [P, 2, CT, 2 * S], F32R, ft)
            gact = sb("gact", [P, 2, 2 * S], F32, ft)
            inter = sb("inter", [P, 2, 2 * S], F32, ft)
            in_hi = sb("in_hi", [P, 2, 2 * S], F32R, ft)
            in_lo = sb("in_lo", [P, 2, 2 * S], F32R, ft)
            causal01 = sb("causal01", [P, TB, S], F32, ft)
            gw_row = sb("gw_row", [P, D], F32, ft)
            win = sb("win", [GR, 6, S], F32, ft)
            val_hi = sb("val_hi", [P, 2, TB, 2 * D], F32R, ft)
            val_lo = sb("val_lo", [P, 2, TB, 2 * D], F32R, ft)
            gT_hi = sb("gT_hi", [P, 2, CT, S], F32R, ft)
            gT_lo = sb("gT_lo", [P, 2, CT, S], F32R, ft)
            qk_hi = sb("qk_hi", [GR, 2, S], F32R, ft)
            qk_lo = sb("qk_lo", [GR, 2, S], F32R, ft)
            am_hi = sb("am_hi", [P, TB, S], F32R, ft)
            am_lo = sb("am_lo", [P, TB, S], F32R, ft)
            junk = sb("junk", [P, D], F32, ft)
            ssq = sb("ssq", [P, TB], F32, ft)
            vs = sb("vs", [P, TB], F32, ft)
            rr = sb("rr", [P, TB], F32, ft)
        row = iter(range(3 * MT))

        def gwork(n, parts=P):
            r = next(row)
            for _ in range(n - 1):
                next(row)
            return spline[0:parts, r:r + n, :]

        gx0, gx1, am, rms, gact_o = (gwork(2) for _ in range(5))
        gx = (gx0, gx1)
        qk = gwork(2, GR)
        qs, kt, ks, dt, dec, qwn, kwn, dq, dk, fq, fk = (gwork(1, GR)[:, 0] for _ in range(11))

        heads = nc.dram_tensor("heads", [2, 2, 4, HH, DK, S], F32, kind="Internal").ap()

        s_x = [sem(f"x_loaded{n}") for n in range(4)]
        s_w = sem("weights_loaded")
        s_cp = sem("control_points_loaded")
        s_ident = sem("ident_made")
        s_const = sem("constants_made")
        s_stack, s_stack0 = sem("stack_rows_set"), sem("stack_first_rows_set")
        s_prep_ps, s_prep_hi, s_prep_lo = sem("prep_turned"), sem("prep_high"), sem("prep_low")
        s_fturn, s_fhi, s_flo = sem("spline_turned"), sem("spline_high"), sem("spline_low")
        s_gc, s_gload = sem("gla_constants_made"), sem("gla_constants_loaded")
        per = {}

        def counted(name, n):
            s = sem(name)
            per[s.name] = n
            return s

        a_bn, a_mv, a_ve = counted("a_bn", 2), counted("a_mv", 2), counted("a_ve", 1)
        a_xn = counted("a_xn", 2)
        a_xl = counted("a_xl", 1)
        a_qkl = counted("a_qkl", 2)
        a_mx = counted("a_mx", NP)
        a_m = counted("a_m", 4)
        a_mh, a_ml = counted("a_mh", 2), counted("a_ml", 2)
        a_rd, a_at = counted("a_rd", 2), counted("a_at", 2)
        a_atl = counted("a_atl", 1)
        a_res = counted("a_res", 1)
        by_dve = [a_bn, a_mv, a_ve, a_xn, a_xl, a_qkl, a_mx, a_m, a_mh, a_ml, a_rd, a_at, a_atl, a_res]
        a_rs, a_pm = counted("a_rs", 1), counted("a_pm", NP)
        a_sp4 = counted("a_spl", 9)
        by_pool = [a_rs, a_pm, a_sp4]
        a_xh, a_qkh = counted("a_xh", 1), counted("a_qkh", 2)
        a_v, a_e = counted("a_v", 1), counted("a_e", NP)
        a_o, a_ath = counted("a_o", 2), counted("a_ath", 1)
        a_pr = counted("a_pr", 3)
        by_act = [a_pr, a_xh, a_qkh, a_v, a_e, a_o, a_ath]
        a_xT, a_qkp, a_vp = counted("a_xT", 1), counted("a_qkp", 2), counted("a_vp", 1)
        a_sp, a_mT, a_stp = counted("a_sp", NP), counted("a_mT", 2), counted("a_stp", NP)
        a_pv, a_ot, a_atT, a_y = counted("a_pv", NP), counted("a_ot", 2), counted("a_atT", 1), counted("a_y", 1)
        by_pe = [a_xT, a_qkp, a_vp, a_sp, a_mT, a_stp, a_pv, a_ot, a_atT, a_y]
        N_STACK = 4
        a_wr = [counted(f"a_wr{h}", 16) for h in range(2)]
        a_stk = [counted(f"a_stk{h}", 16 * N_STACK) for h in range(2)]
        a_md = [counted(f"a_md{h}", 32) for h in range(2)]
        a_phi = counted("a_phi", 16)
        passed_dve, passed_pool = sem("passed_dve"), sem("passed_pool")
        passed_act, passed_sp = sem("passed_act"), sem("passed_sp")
        s_out = sem("out_stored")

        def ffn_semaphores(tag):
            f = Signals()

            def own(n, count):
                return counted(f"{tag}_{n}", count)

            f.bn, f.mv, f.ve, f.xn, f.xl = own("bn", 4), own("mv", 4), own("ve", 1), own("xn", 4), own("xl", 2)
            f.up, f.il, f.res = own("up", MT), own("il", MT), own("res", 2)
            f.dve = [f.bn, f.mv, f.ve, f.xn, f.xl, f.up, f.il, f.res]
            f.rs = own("rs", 1)
            f.pool = [f.rs]
            f.xh, f.si, f.ih = own("xh", 2), own("si", MT), own("ih", MT)
            f.act = [f.xh, f.si, f.ih]
            f.xT, f.gp, f.upp, f.dp = own("xT", 2), own("gp", MT), own("upp", MT), own("dp", MT)
            f.pe = [f.xT, f.gp, f.upp, f.dp]
            return f

        f1, f2 = ffn_semaphores("f1"), ffn_semaphores("f2")

        def gla_semaphores():
            f = Signals()

            def own(n, count=1):
                return counted(f"g_{n}", count)

            f.bn, f.mv, f.nm, f.ve, f.xl = own("bn", 2), own("mv", 2), own("nm"), own("ve"), own("xl")
            f.sf, f.rc, f.sb, f.qd, f.kd, f.qkl = own("sf"), own("rc"), own("sb"), own("qd"), own("kd"), own("qkl")
            f.am, f.aml, f.wl, f.vs = own("am"), own("aml"), own("wl"), own("vs")
            f.dve = [f.bn, f.mv, f.nm, f.ve, f.xl, f.sf, f.rc, f.sb, f.qd, f.kd, f.qkl, f.am, f.aml, f.wl, f.vs]
            f.rs, f.mr, f.gl, f.w = own("rs"), own("mr"), own("gl"), own("w", 4)
            f.rr, f.mu, f.res = own("rr"), own("mu", 2), own("res")
            f.pool = [f.rs, f.mr, f.gl, f.w, f.rr, f.mu, f.res]
            f.xn, f.xh, f.gh, f.qs, f.kt, f.ks = own("xn", 2), own("xh"), own("gh"), own("qs"), own("kt"), own("ks")
            f.dt, f.de, f.qkh, f.amh = own("dt"), own("de"), own("qkh"), own("amh")
            f.wh, f.sq, f.rm, f.gs = own("wh"), own("sq", 2), own("rm", 2), own("gs")
            f.act = [f.xn, f.xh, f.gh, f.qs, f.kt, f.ks, f.dt, f.de, f.qkh, f.amh, f.wh, f.sq, f.rm, f.gs]
            f.xT, f.qk, f.xw, f.ap, f.gi, f.o = own("xT"), own("qk"), own("xw"), own("ap"), own("gi"), own("o", 2)
            f.pe = [f.xT, f.qk, f.xw, f.ap, f.gi, f.o]
            return f

        g_ = gla_semaphores()

        def lead(eng, owned):
            for s in owned:
                eng.sem_inc(s, LEAD * per[s.name])

        def upto(s, b, k):
            return per[s.name] * (b + LEAD) + k

        def mm3(pe, dst, l_hi, l_lo, r_hi, r_lo, first, last):
            pe.matmul(dst, l_hi, r_hi, start=first, stop=False)
            pe.matmul(dst, l_hi, r_lo, start=False, stop=False)
            return pe.matmul(dst, l_lo, r_hi, start=False, stop=last)

        phi_t = phi.rearrange("j p (m c) -> j p m c", m=WIN)
        x_t = x.rearrange("b (t p) c -> p (b t) c", p=P)
        out_t = out.rearrange("b (t p) c -> p (b t) c", p=P)
        bank_y4 = bank_y[:, :].rearrange("p (t h w) -> p t h w", t=TB, h=HH)
        def run_periods(eng, period):
            period(0, 0, 0, prev=False)
            period(1, 0, 1)
            with eng.Fori(1, B // 2 - 2) as j:
                period(2 * j, j, 0)
                period(2 * j + 1, j, 1)
            period(B - 4, B // 2 - 2, 0)
            period(B - 3, B // 2 - 2, 1, nxt3=False)
            period(B - 2, B // 2 - 1, 0, nxt2=False, nxt3=False)
            period(B - 1, B // 2 - 1, 1, nxt=False, nxt2=False, nxt3=False)

        PAIRS = B // 2

        def run_pairs(period):
            def run(eng):
                period(0, 0, prev=False)
                with eng.Fori(0, PAIRS // 2 - 1) as j:
                    period(2 * j + 1, 1)
                    period(2 * j + 2, 0)
                period(PAIRS - 1, 1, nxt=False)
            return run

        def run_gla(eng, period):
            period(0, 0, prev=False, prev2=False)
            period(1, 1, prev2=False)
            with eng.Fori(1, B // 2 - 2) as j:
                period(2 * j, 0)
                period(2 * j + 1, 1)
            period(B - 4, 0)
            period(B - 3, 1, nxt3=False)
            period(B - 2, 0, nxt3=False, nxt2=False)
            period(B - 1, 1, nxt3=False, nxt2=False, nxt=False)
            period(B, 0, nxt3=False, nxt2=False, nxt=False, cur=False)

        def turned_down(t):
            return t.rearrange("p (c x q) -> p c q x", c=CT, q=4)

        def out_bank(u, q):
            return (pair_b[:, q, :], (bank_o, bank_y)[q][:, :])[u]

        block = outer.enter_context(nc.Block())

        @block.sync
        def _(sp):
            sp.dma_start(X[:, 0:TB, :], x_t[:, 0:TB, :]).then_inc(s_x[0], 16)
            for n, w in enumerate((a_wq, a_wk, a_wv, a_wo, b_wog, b_wig)):
                sp.dma_start(wnat[:, n], w.rearrange("(o p) c -> p o c", p=P)).then_inc(s_w, 16)
            for n, w in enumerate((b_wq, b_wk)):
                sp.dma_start(bnat[:, n, :], w).then_inc(s_w, 16)
            sp.dma_start(X[:, TB:2 * TB, :], x_t[:, TB:2 * TB, :]).then_inc(s_x[1], 16)
            sp.dma_start(basis[:, 0], phi_t[0, :, :, 0:P]).then_inc(a_phi, 16)
            for w in range(3):
                for half in range(2):
                    window = bass.AP(tensor=cps.tensor, offset=w * N_CP + 127 * half,
                                     ap=[[2, 64], [254, MT], [1, WIN]])
                    sp.dma_start(cpw[64 * half:64 * half + 64, w], window).then_inc(s_cp, 16)
            sp.dma_start(X[:, 2 * TB:4 * TB, :], x_t[:, 2 * TB:4 * TB, :]).then_inc(s_x[2], 16)
            lead(sp, a_stk + a_md + a_wr + [a_phi])

            def stack_half(b, u, h, after_use=True):
                sp.wait_ge(a_qkh, upto(a_qkh, b, h + 1))
                sp.sem_inc(passed_sp, 1)
                sp.wait_ge(a_qkl, upto(a_qkl, b, h + 1))
                sp.sem_inc(passed_sp, 1)
                if after_use:
                    sp.wait_ge(a_stp, upto(a_stp, b - 2, 4 * h + 4))
                sp.dma_start(heads[u, h].rearrange("n h d t -> (h d) n t"),
                             stage[:, h].bitcast(F32)).then_inc(a_wr[h], 16)
                sp.wait_ge(a_wr[h], upto(a_wr[h], b, 16))
                for r in range(2):
                    sp.dma_start(stack[DK * r:DK * r + DK, u, h].bitcast(F32),
                                 heads[u, h, 2 * r:2 * r + 2].rearrange("n h d t -> d (n h) t")).then_inc(a_stk[h], 16)
                for n in range(2):
                    sp.dma_start(stack[2 * DK:3 * DK, u, h, n].bitcast(F32),
                                 heads[u, h, 3 * n].rearrange("h d t -> d h t")).then_inc(a_stk[h], 16)

            def max_rows(b, u, h):
                sp.wait_ge(a_ml, upto(a_ml, b, h + 1))
                for n in range(2):
                    sp.dma_start(stack[MROW + n:MROW + n + 1, u, h, 0, :, :].bitcast(F32),
                                 mrow[:, h, n, :].bitcast(F32)).then_inc(a_md[h], 16)

            for b in range(2):
                for h in range(2):
                    if b or h:
                        sp.wait_ge(s_stack, 4 * b + 2 * h)
                    else:
                        sp.wait_ge(s_stack0, 2)
                    if b and h:
                        max_rows(0, 0, 0)
                    stack_half(b, b, h, False)
            sp.dma_start(X[:, 4 * TB:, :], x_t[:, 4 * TB:, :]).then_inc(s_x[3], 16)

            def period(b, j, u, prev=True, nxt=True, nxt2=True, nxt3=True):
                max_rows(b, u, 1)
                if nxt:
                    sp.wait_ge(a_sp4, upto(a_sp4, b - 1, 9))
                    sp.sem_inc(passed_sp, 1)
                    tile = j + u
                    sp.dma_start(basis[:, 1 - u], phi_t[bass.ds(tile, 1), :, :, (1 - u) * P:(1 - u) * P + P]
                                 .rearrange("j p m c -> (j p) m c")).then_inc(a_phi, 16)
                if nxt2:
                    stack_half(b + 2, u, 0)
                if nxt:
                    max_rows(b + 1, 1 - u, 0)
                if nxt2:
                    stack_half(b + 2, u, 1)

            run_periods(sp, period)
            sp.wait_ge(s_fturn, 1)
            sp.dma_start(gw_row[:, :], g_weight.rearrange("(o c) -> o c", o=1).to_broadcast([P, D])
                         ).then_inc(s_gload, 16)
            sp.dma_start(win[:, :, :], windows).then_inc(s_gload, 16)
            with sp.Fori(0, PAIRS) as g:
                sp.wait_ge(f2.res, upto(f2.res, g, 2))
                sp.dma_start(out_t[:, bass.ds(2 * TB * g, 2 * TB), :],
                             X[:, bass.ds(2 * TB * g, 2 * TB), :]).then_inc(s_out, 16)
            sp.wait_ge(s_out, 16 * PAIRS)

        @block.gpsimd
        def _(pool):
            pool.memset(ident[:, :], 0.0).then_inc(s_ident, 1)
            pool.wait_ge(s_ident, 1)
            pool.affine_select(out=ident[:, :], in_=ident[:, :], compare_op=ALU.not_equal, fill=1.0, base=0,
                               pattern=[[-1, P]], channel_multiplier=1).then_inc(s_ident, 1)
            lead(pool, by_pool + f1.pool + f2.pool + g_.pool)
            pool.memset(causal_neg[:, :, :], 0.0).then_inc(s_const, 1)
            pool.memset(half_neg[:, :, :], -0.5).then_inc(s_const, 1)
            pool.memset(quarter[:, :], 0.25).then_inc(s_const, 1)
            pool.memset(V[:, :, :, :, DK:DK + 1], 1.0).then_inc(s_const, 1)
            pool.memset(V[:, :, :, :, DK + 1:32], 0.0).then_inc(s_const, 1)
            pool.wait_ge(s_const, 5)
            pool.affine_select(out=causal_neg[:, :, :], in_=causal_neg[:, :, :], compare_op=ALU.is_ge,
                               fill=NEG, base=0, pattern=[[0, 2], [-1, P]],
                               channel_multiplier=1).then_inc(s_const, 1)
            pool.wait_ge(s_ident, 2)
            pool.tensor_copy(ident16[:, :], ident[:, :]).then_inc(s_const, 1)

            def rstd(b, u):
                pool.wait_ge(a_ve, upto(a_ve, b, 1))
                pool.tensor_tensor(rs[:, u, :], ve[:, u, :], half_neg[:, 0, :], ALU.pow).then_inc(a_rs, 1)

            def mask(b, p):
                pool.wait_ge(a_e, upto(a_e, b, p + 1))
                pool.sem_inc(passed_pool, 1)
                diag = prob[:, p % 2, :, 0:2 * P].rearrange("p h (t q) -> p h t q", t=2)
                pool.affine_select(out=diag, in_=diag, compare_op=ALU.is_ge, fill=0.0, base=0,
                                   pattern=[[0, 2], [0, 2], [1, P]], channel_multiplier=-1).then_inc(a_pm, 1)

            def spline_rows(b, j, u, w):
                steps = 3 * w
                pool.wait_ge(a_pr, upto(a_pr, b, w + 1))
                pool.tensor_tensor(prod[:, 0:3], prod[:, 0:3], prod[:, 3:6], ALU.add).then_inc(a_sp4, 1)
                pool.wait_ge(a_sp4, upto(a_sp4, b, steps + 1))
                pool.tensor_tensor(prod[:, 0], prod[:, 0], prod[:, 1], ALU.add).then_inc(a_sp4, 1)
                pool.wait_ge(a_sp4, upto(a_sp4, b, steps + 2))
                pool.sem_inc(passed_pool, 1)
                pool.tensor_tensor(spline[:, bass.ds(MT * w + j, 1), P * u:P * u + P], prod[:, 0:1],
                                   prod[:, 2:3], ALU.add).then_inc(a_sp4, 1)

            def stack_rows(u, h, n):
                rows = stack[:, u, h].bitcast(F32)
                pool.memset(rows, 0.0).then_inc(s_stack, 1)
                pool.wait_ge(s_stack, 2 * n - 1)
                pool.memset(rows[64:K_ST, 1], 1.0).then_inc(s_stack, 1)
                pool.wait_ge(s_stack, 2 * n)

            stack_rows(0, 1, 1)
            rstd(0, 0)
            stack_rows(1, 0, 2)
            rstd(1, 1)
            stack_rows(1, 1, 3)
            rstd(2, 0)
            pool.wait_ge(s_prep_lo, 7)

            def period(b, j, u, prev=True, nxt=True, nxt2=True, nxt3=True):
                for p in range(NP):
                    mask(b, p)
                    if p == 4 and nxt3:
                        rstd(b + 3, 1 - u)
                    if p in (2, 4, 7):
                        spline_rows(b, j, u, p // 3)

            run_periods(pool, period)

            def ffn(f):
                def rstd4(g):
                    pool.wait_ge(f.ve, upto(f.ve, g, 1))
                    pool.tensor_tensor(rs[:, :, :], ve[:, :, :], half_neg[:, :, :], ALU.pow).then_inc(f.rs, 1)

                def run():
                    with pool.Fori(1, PAIRS) as g:
                        rstd4(g)

                return rstd4, run

            def g_rstd(n, u):
                pool.wait_ge(g_.ve, upto(g_.ve, n, 1))
                pool.tensor_tensor(rs[:, u, :], ve[:, u, :], half_neg[:, 0, :], ALU.pow).then_inc(g_.rs, 1)
                pool.wait_ge(g_.rs, upto(g_.rs, n, 1))
                pool.tensor_tensor(nmr[:, u, :], negm[:, u, :], rs[:, u, :], ALU.mult).then_inc(g_.mr, 1)

            def g_low_x(n, u):
                pool.wait_ge(g_.gh, upto(g_.gh, n, 1))
                pool.tensor_tensor(val_lo[:, u, :, 0:D], gx[u], val_hi[:, u, :, 0:D].bitcast(F32),
                                   ALU.subtract).then_inc(g_.gl, 1)

            def g_windows(n):
                pool.wait_ge(g_.qs, upto(g_.qs, n, 1))
                pool.wait_ge(g_.qd, upto(g_.qd, n - 1, 1))
                pool.tensor_tensor(qwn, qs, win[:, 4], ALU.mult).then_inc(g_.w, 1)
                pool.wait_ge(g_.ks, upto(g_.ks, n, 1))
                pool.wait_ge(g_.kd, upto(g_.kd, n - 1, 1))
                pool.tensor_tensor(kwn, ks, win[:, 5], ALU.mult).then_inc(g_.w, 1)
                pool.wait_ge(g_.de, upto(g_.de, n, 1))
                pool.wait_ge(g_.sf, upto(g_.sf, n - 1, 1))
                pool.tensor_tensor(dq, dec, win[:, 0], ALU.mult).then_inc(g_.w, 1)
                pool.wait_ge(g_.sb, upto(g_.sb, n - 1, 1))
                pool.tensor_tensor(dk[:, 0:S - 1], dec[:, 1:S], win[:, 2, 0:S - 1], ALU.mult).then_inc(g_.w, 1)

            def g_rr(n):
                pool.wait_ge(g_.vs, upto(g_.vs, n, 1))
                pool.wait_ge(g_.rm, upto(g_.rm, n - 1, 2))
                pool.tensor_tensor(rr[:, :], vs[:, :], half_neg[:, 0, :], ALU.pow).then_inc(g_.rr, 1)

            def g_residual(n):
                pool.wait_ge(g_.rm, upto(g_.rm, n, 2))
                pool.tensor_tensor(rms, rms, gw_row[:, :].rearrange("p (o c) -> p o c", o=1).to_broadcast([P, TB, D]),
                                   ALU.mult).then_inc(g_.mu, 1)
                pool.wait_ge(g_.mu, upto(g_.mu, n, 1))
                pool.wait_ge(g_.gs, upto(g_.gs, n, 1))
                pool.tensor_tensor(rms, rms, gact_o, ALU.mult).then_inc(g_.mu, 1)
                pool.wait_ge(g_.mu, upto(g_.mu, n, 2))
                pool.sem_inc(passed_pool, 1)
                tok = X[:, bass.ds(TB * n, TB), :]
                pool.tensor_tensor(tok, tok, rms, ALU.add).then_inc(g_.res, 1)

            def gla():
                g_rstd(0, 0)
                g_rstd(1, 1)
                pool.wait_ge(s_gload, 32)
                g_rstd(2, 0)
                g_windows(0)
                g_low_x(0, 0)

                def period(n, u, prev2=True, prev=True, cur=True, nxt=True, nxt2=True, nxt3=True):
                    if prev2:
                        g_residual(n - 2)
                    if nxt3:
                        g_rstd(n + 3, 1 - u)
                    if nxt:
                        g_windows(n + 1)
                    if prev:
                        g_rr(n - 1)
                    if nxt:
                        g_low_x(n + 1, 1 - u)
                    if nxt and not nxt2:
                        f2_rstd(0)

                run_gla(pool, period)
                g_residual(B - 1)

            f1_rstd, run_f1 = ffn(f1)
            f2_rstd, run_f2 = ffn(f2)
            f1_rstd(0)
            pool.wait_ge(s_fturn, 1)
            pool.memset(causal01[:, :, :], 1.0).then_inc(s_gc, 1)
            pool.wait_ge(s_gc, 1)
            pool.affine_select(out=causal01[:, 0, 0:P], in_=causal01[:, 0, 0:P], compare_op=ALU.is_ge, fill=0.0,
                               base=0, pattern=[[1, P]], channel_multiplier=-1).then_inc(s_gc, 1)
            pool.affine_select(out=causal01[:, 1, :], in_=causal01[:, 1, :], compare_op=ALU.is_ge, fill=0.0,
                               base=-P, pattern=[[1, S]], channel_multiplier=-1).then_inc(s_gc, 1)
            pool.wait_ge(s_flo, 3 * MT // 2)
            pool.memset(dk[:, S - 1:S], 0.0).then_inc(s_gc, 1)
            run_f1()
            gla()
            run_f2()

        @block.tensor
        def _(pe):
            lead(pe, by_pe + f1.pe + f2.pe + g_.pe)
            pe.wait_ge(s_ident, 2)
            pe.wait_ge(s_w, 16 * 8)
            for n in range(6):
                dst = prep_bank[n][:, :].rearrange("p (c o) -> p c o", c=CT)
                for o in range(CT):
                    for c in range(CT):
                        t = pe.transpose(dst[:, c, P * o:P * o + P], wnat[:, n, o, P * c:P * c + P], ident[:, :])
                t.then_inc(s_prep_ps, 1)
            for n in range(2):
                for c in range(CT):
                    t = pe.transpose(prep_bank[6][:, KG * (2 * n + c):KG * (2 * n + c) + KG],
                                     bnat[:, n, P * c:P * c + P], ident[0:KG, 0:KG])
            t.then_inc(s_prep_ps, 1)
            pe.wait_ge(s_prep_lo, 2)

            def turn_x(b, u):
                pe.wait_ge(a_xn, upto(a_xn, b, 2))
                for c in range(CT):
                    for t in range(TB):
                        i = pe.transpose(bank_t[:, S * c + P * t:S * c + P * t + P], xn[:, t, P * c:P * c + P], ident[:, :])
                i.then_inc(a_xT, 1)

            def proj_qk(b, u, h):
                for n, w in enumerate((wq, wk)):
                    for c in range(CT):
                        cols = slice(P * h, P * h + P)
                        i = mm3(pe, bank_p[:, S * n:S * n + S], w[0][:, c, cols], w[1][:, c, cols],
                                xT_hi[:, u, c, :], xT_lo[:, u, c, :], c == 0, c == CT - 1)
                i.then_inc(a_qkp, 1)

            def proj_v(b, u):
                for t in range(TB):
                    for c in range(CT):
                        tok = slice(P * t, P * t + P)
                        i = mm3(pe, bank_y[:, D * t:D * t + D], xT_hi[:, u, c, tok], xT_lo[:, u, c, tok],
                                wv[0][:, c, :], wv[1][:, c, :], c == 0, c == CT - 1)
                i.then_inc(a_vp, 1)

            def scores(b, u, p, both=False):
                h = p // 4
                if p % 4 == 0:
                    pe.wait_ge(a_stk[h], upto(a_stk[h], b, 16 * N_STACK))
                pe.wait_ge(a_mx, upto(a_mx, b, p - both))
                dst = pair_a if both and p % 2 else pair_b
                for n in range(2):
                    hd = (2 * p + n) % HH
                    for t, at_col in ((1, 0), (0, S)):
                        pe.matmul(dst[:, n, at_col:at_col + S], stack[0:K_S, u, h, 0, hd, P * t:P * t + P],
                                  stack[0:K_S, u, h, 1, hd, :], start=(t == 1), stop=False)
                    i = pe.matmul(dst[:, n, P:3 * P], ident16[:, :],
                                  causal_neg[:, :, :].rearrange("p a b -> p (a b)"), start=False, stop=True)
                i.then_inc(a_sp, 1)

            def turn_max(b, h):
                pe.wait_ge(a_m, upto(a_m, b, 2 * h + 2))
                for t in range(TB):
                    i = pe.transpose(bank_t[0:HH, P * t:P * t + P], mx2[:, h, t, :], ident[:, :])
                i.then_inc(a_mT, 1)

            def shifted(b, u, p):
                h = p // 4
                if p % 4 == 0:
                    pe.wait_ge(a_md[h], upto(a_md[h], b, 32))
                pe.wait_ge(a_e, upto(a_e, b, p))
                for n in range(2):
                    hd = (2 * p + n) % HH
                    for t, at_col in ((1, 0), (0, S)):
                        i = pe.matmul(pair_a[:, n, at_col:at_col + S], stack[0:K_ST, u, h, 1, hd, P * t:P * t + P],
                                      stack[0:K_ST, u, h, 0, hd, :], start=True, stop=True)
                i.then_inc(a_stp, 1)

            def weigh(b, u, p):
                pe.wait_ge(a_pm, upto(a_pm, b, p + 1))
                if p == 0:
                    pe.wait_ge(a_v, upto(a_v, b, 1))
                if p % 4 == 0:
                    pe.wait_ge(a_o, upto(a_o, b, p // 4))
                g = (p % 4) // 2
                for n in range(2):
                    at = 32 * ((2 * p + n) % 4)
                    pe.matmul(bank_o[at:at + 32, S * g:S * g + S], V[:, u, 0, 2 * p + n, :],
                              prob[:, p % 2, n, P:3 * P], start=True, stop=False, tile_position=(0, at))
                for n in range(2):
                    at = 32 * ((2 * p + n) % 4)
                    i = pe.matmul(bank_o[at:at + 32, S * g + P:S * g + S], V[:, u, 1, 2 * p + n, :],
                                  prob[:, p % 2, n, 0:P], start=False, stop=True, tile_position=(0, at))
                i.then_inc(a_pv, 1)

            def turn_o(b, h):
                pe.wait_ge(a_o, upto(a_o, b, h + 1))
                for t in range(TB):
                    for g in range(2):
                        i = pe.transpose(bank_y[:, S * t + P * g:S * t + P * g + P], oT[:, h, g, P * t:P * t + P],
                                         ident[:, :])
                i.then_inc(a_ot, 1)

            def turn_att(b):
                pe.wait_ge(a_at, upto(a_at, b, 2))
                for c in range(CT):
                    for t in range(TB):
                        i = pe.transpose(bank_t[:, S * c + P * t:S * c + P * t + P], att[:, t, P * c:P * c + P], ident[:, :])
                i.then_inc(a_atT, 1)

            def proj_out(b):
                pe.wait_ge(a_atl, upto(a_atl, b, 1))
                for t in range(TB):
                    for c in range(CT):
                        tok = slice(P * t, P * t + P)
                        i = mm3(pe, bank_p[:, D * t:D * t + D], attT_hi[:, c, tok], attT_lo[:, c, tok],
                                wo[0][:, c, :], wo[1][:, c, :], c == 0, c == CT - 1)
                i.then_inc(a_y, 1)

            for b in range(2):
                if b:
                    pe.wait_ge(a_xl, upto(a_xl, b - 1, 1))
                turn_x(b, b)
                pe.wait_ge(a_xl, upto(a_xl, b, 1))
                if b:
                    pe.wait_ge(a_qkl, upto(a_qkl, b - 1, 2))
                proj_qk(b, b, 0)
                pe.wait_ge(a_qkl, upto(a_qkl, b, 1))
                if b == 0:
                    proj_qk(b, b, 1)
                else:
                    pe.wait_ge(s_prep_lo, 7)
                    pe.wait_ge(s_const, 7)
                    for p in range(4):
                        scores(0, 0, p, both=True)
                    turn_max(0, 0)
                    proj_qk(b, b, 1)
                    for p in range(4, NP):
                        scores(0, 0, p, both=True)
                if b == 0:
                    pe.wait_ge(s_prep_lo, 4)
                    proj_v(0, 0)
            pe.wait_ge(a_mx, upto(a_mx, 0, NP))

            def period(b, j, u, prev=True, nxt=True, nxt2=True, nxt3=True):
                for p in range(NP):
                    shifted(b, u, p)
                    if p or prev:
                        weigh(b if p else b - 1, u if p else 1 - u, (p - 1) % NP)
                    if p == 0 and nxt2:
                        pe.wait_ge(a_ml, upto(a_ml, b, 1))
                        turn_x(b + 2, u)
                    if p == 1:
                        if nxt2:
                            pe.wait_ge(a_xl, upto(a_xl, b + 2, 1))
                        else:
                            pe.wait_ge(a_ml, upto(a_ml, b, 1))
                        turn_max(b, 1)
                    if p == 2 and prev:
                        pe.wait_ge(a_at, upto(a_at, b - 1, 1))
                        turn_o(b - 1, 1)
                    if p == 3:
                        if prev:
                            pe.wait_ge(a_ml, upto(a_ml, b, 2))
                            turn_att(b - 1)
                        if nxt2:
                            pe.wait_ge(a_xl, upto(a_xl, b + 2, 1))
                            pe.wait_ge(a_res, upto(a_res, b - 2, 1))
                            pe.wait_ge(a_qkl, upto(a_qkl, b + 1, 2))
                            proj_qk(b + 2, u, 0)
                    if p == 4 and nxt:
                        pe.wait_ge(a_at, upto(a_at, b - 1, 2))
                        if not prev:
                            pe.wait_ge(a_v, upto(a_v, 0, 1))
                        proj_v(b + 1, 1 - u)
                    if p == 5:
                        if nxt2:
                            pe.wait_ge(a_qkl, upto(a_qkl, b + 2, 1))
                            proj_qk(b + 2, u, 1)
                        if nxt:
                            pe.wait_ge(a_ml, upto(a_ml, b, 2))
                            pe.wait_ge(a_atl, upto(a_atl, b - 1, 1))
                            turn_max(b + 1, 0)
                    if p == 6:
                        if nxt:
                            pe.wait_ge(a_v, upto(a_v, b + 1, 1))
                        else:
                            pe.wait_ge(a_at, upto(a_at, b - 1, 2))
                        turn_o(b, 0)
                    if p == 7 and prev:
                        if nxt2:
                            pe.wait_ge(a_qkl, upto(a_qkl, b + 2, 2))
                        pe.wait_ge(a_res, upto(a_res, b - 2, 1))
                        proj_out(b - 1)
                    if nxt:
                        scores(b + 1, 1 - u, p)

            run_periods(pe, period)
            weigh(B - 1, 1, NP - 1)
            pe.wait_ge(a_at, upto(a_at, B - 1, 1))
            turn_o(B - 1, 1)
            turn_att(B - 1)
            pe.wait_ge(a_res, upto(a_res, B - 2, 1))
            proj_out(B - 1)

            def turn_spline(fills):
                for n in fills:
                    if n >= 8:
                        pe.wait_ge(s_flo, n - 7)
                    for c in range(CT):
                        for r in range(2):
                            i = pe.transpose(fill_bank[n % 8][:, 2 * P * c + P * r:2 * P * c + P * r + P],
                                             spline[:, 2 * n + r, P * c:P * c + P], ident[:, :])
                    i.then_inc(s_fturn, 1)

            def ffn(f, tail):
                def turn_in(g, h):
                    pe.wait_ge(f.xn, upto(f.xn, g, 4))
                    pe.wait_ge(f.xl, upto(f.xl, g, h))
                    for c in range(CT):
                        for t in range(TB):
                            i = pe.transpose(bank_t[:, S * c + P * t:S * c + P * t + P],
                                             xn_f[:, TB * h + t, P * c:P * c + P], ident[:, :])
                    i.then_inc(f.xT, 1)

                def inner(dst, w_hi, w_lo, u, m):
                    cols = slice(P * m, P * m + P)
                    for c in range(CT):
                        i = mm3(pe, dst, w_hi[:, c, cols], w_lo[:, c, cols], fT_hi[:, u, c, :], fT_lo[:, u, c, :],
                                c == 0, c == CT - 1)
                    return i

                def down(g, m):
                    pe.wait_ge(f.il, upto(f.il, g, m + 1))
                    if m == 0:
                        pe.wait_ge(f.res, upto(f.res, g - 1, 2))
                    for t in range(2 * TB):
                        tok = slice(P * t, P * t + P)
                        dst = (bank_o, bank_y)[t // TB][:, D * (t % TB):D * (t % TB) + D]
                        i = mm3(pe, dst, in_hi[:, m % 2, tok], in_lo[:, m % 2, tok], wd_hi[:, m, :], wd_lo[:, m, :],
                                m == 0 and t % TB == 0, m == MT - 1 and t % TB == TB - 1)
                    i.then_inc(f.dp, 1)

                def period(g, u, prev=True, nxt=True):
                    pe.wait_ge(f.xl, upto(f.xl, g, 2))
                    for m in range(MT):
                        pe.wait_ge(f.si, upto(f.si, g, m - 1))
                        inner(pair_a[:, m % 2, :], wg_hi, wg_lo, u, m).then_inc(f.gp, 1)
                        pe.wait_ge(f.up, upto(f.up, g, m - 1))
                        inner(pair_b[:, m % 2, :], wu_hi, wu_lo, u, m).then_inc(f.upp, 1)
                        if m or prev:
                            down(g if m else g - 1, (m - 1) % MT)
                        if m in (4, 5) and nxt:
                            turn_in(g + 1, m - 4)
                        if not nxt:
                            tail(m)

                def run():
                    run_pairs(period)(pe)
                    down(PAIRS - 1, MT - 1)

                return turn_in, run

            def g_turn(n, u):
                pe.wait_ge(g_.xn, upto(g_.xn, n, 2))
                pe.wait_ge(g_.xl, upto(g_.xl, n - 1, 1))
                for c in range(CT):
                    for t in range(TB):
                        i = pe.transpose(bank_t[:, S * c + P * t:S * c + P * t + P], gx[u][:, t, P * c:P * c + P],
                                         ident[:, :])
                i.then_inc(g_.xT, 1)

            def g_project(n, u):
                pe.wait_ge(g_.xl, upto(g_.xl, n, 1))
                pe.wait_ge(g_.qs, upto(g_.qs, n - 1, 1))
                pe.wait_ge(g_.kt, upto(g_.kt, n - 1, 1))
                for w in range(2):
                    for c in range(CT):
                        i = mm3(pe, bank_p[0:GR, S * w:S * w + S], wqk_hi[:, w, c, :], wqk_lo[:, w, c, :],
                                gT_hi[:, u, c, :], gT_lo[:, u, c, :], c == 0, c == CT - 1)
                i.then_inc(g_.qk, 1)

            def g_products(n):
                pe.wait_ge(g_.qkl, upto(g_.qkl, n, 1))
                pe.wait_ge(g_.am, upto(g_.am, n - 1, 1))
                for t in range(TB):
                    keys = slice(P * t, P * t + P)
                    i = mm3(pe, pair_a[:, 0, S * t:S * t + S], qk_hi[:, 1, keys], qk_lo[:, 1, keys],
                            qk_hi[:, 0, :], qk_lo[:, 0, :], True, True)
                i.then_inc(g_.ap, 1)

            def g_values(n, u):
                pe.wait_ge(g_.xl, upto(g_.xl, n, 1))
                pe.wait_ge(g_.wl, upto(g_.wl, n - 1, 1))
                for t in range(TB):
                    for c in range(CT):
                        tok = slice(P * t, P * t + P)
                        i = mm3(pe, pair_a[:, 1, D * t:D * t + D], gT_hi[:, u, c, tok], gT_lo[:, u, c, tok],
                                wog[0][:, c, :], wog[1][:, c, :], c == 0, c == CT - 1)
                i.then_inc(g_.xw, 1)

            def g_gate_in(n, u):
                pe.wait_ge(g_.rm, upto(g_.rm, n - 2, 2))
                pe.wait_ge(g_.gs, upto(g_.gs, n - 2, 1))
                for q in range(TB):
                    tok = slice(P * q, P * q + P)
                    for c in range(CT):
                        i = mm3(pe, out_bank(u, q)[:, D:2 * D], gT_hi[:, u, c, tok], gT_lo[:, u, c, tok],
                                wig[0][:, c, :], wig[1][:, c, :], c == 0, False)
                i.then_inc(g_.gi, 1)

            def g_output(n, u):
                pe.wait_ge(g_.gl, upto(g_.gl, n, 1))
                pe.wait_ge(g_.wl, upto(g_.wl, n, 1))
                pe.wait_ge(g_.aml, upto(g_.aml, n, 1))
                for q in range(TB):
                    tok = slice(P * q, P * q + P)
                    for part in range(2):
                        cols = slice(D * part, D * part + D)
                        for t in range(q + 1):
                            i = mm3(pe, out_bank(u, q)[:, cols], am_hi[:, t, tok], am_lo[:, t, tok],
                                    val_hi[:, u, t, cols], val_lo[:, u, t, cols], False, part == 1 and t == q)
                    i.then_inc(g_.o, 1)

            def gla():
                g_values(0, 0)
                pe.wait_ge(f1.res, upto(f1.res, PAIRS - 1, 2))

                def period(n, u, prev2=True, prev=True, cur=True, nxt=True, nxt2=True, nxt3=True):
                    if nxt:
                        g_project(n + 1, 1 - u)
                        g_values(n + 1, 1 - u)
                    if not cur:
                        f2_turn(0, 0)
                    if prev:
                        g_output(n - 1, 1 - u)
                    if not cur:
                        f2_turn(0, 1)
                    if cur:
                        g_gate_in(n, u)
                    if nxt2:
                        g_turn(n + 2, u)
                    if cur:
                        g_products(n)

                run_gla(pe, period)

            def gla_start(m):
                if m == 3:
                    g_turn(0, 0)
                if m == 4:
                    g_project(0, 0)
                if m == 5:
                    g_turn(1, 1)

            f1_turn, run_f1 = ffn(f1, gla_start)
            f2_turn, run_f2 = ffn(f2, lambda m: None)
            pe.wait_ge(a_sp4, upto(a_sp4, B - 1, 9))
            turn_spline(range(6))
            f1_turn(0, 0)
            f1_turn(0, 1)
            pe.wait_ge(f1.xl, upto(f1.xl, 0, 2))
            pe.wait_ge(a_res, upto(a_res, B - 1, 1))
            turn_spline(range(6, 3 * MT // 2))
            pe.wait_ge(s_flo, 3 * MT // 2)
            run_f1()
            gla()
            for n in (B - 2, B - 1):
                pe.wait_ge(g_.rm, upto(g_.rm, n, 2))
                pe.wait_ge(g_.gs, upto(g_.gs, n, 1))
            run_f2()

        @block.scalar
        def _(act):
            lead(act, by_act + f1.act + f2.act + g_.act)

            def prep_dst(n, part):
                return (wq, wk, wv, wo, wog, wig)[n][part][:, :, :]

            for n in range(6):
                act.wait_ge(s_prep_ps, n + 1)
                act.activation(prep_dst(n, 0), prep_bank[n][:, :].rearrange("p (c o) -> p c o", c=CT),
                               ACT.Copy).then_inc(s_prep_hi, 1)
            act.wait_ge(s_prep_ps, 7)
            turned = prep_bank[6][:, 0:4 * KG].rearrange("p (m k) -> p m k", k=KG)
            for g in range(NG):
                act.activation(wqk_hi[:, :, :, KG * g:KG * g + KG].rearrange("p n c k -> p (n c) k"), turned,
                               ACT.Copy).then_inc(s_prep_hi, 1)

            def copy_xT(b, u, used=True):
                act.wait_ge(a_xT, upto(a_xT, b, 1))
                if used:
                    act.wait_ge(a_vp, upto(a_vp, b - 2, 1))
                act.activation(xT_hi[:, u], bank_t[:, :].rearrange("p (c t) -> p c t", c=CT),
                               ACT.Copy).then_inc(a_xh, 1)

            def copy_qk(b, h, used=True):
                act.wait_ge(a_qkp, upto(a_qkp, b, h + 1))
                if used:
                    act.wait_ge(a_stk[h], upto(a_stk[h], b - 1, 16 * N_STACK))
                act.activation(stage[:, h, 0:4:3, :], bank_p[:, :].rearrange("p (n t) -> p n t", n=2),
                               ACT.Copy).then_inc(a_qkh, 1)

            def copy_v(b, u):
                act.wait_ge(a_vp, upto(a_vp, b, 1))
                act.wait_ge(a_pv, upto(a_pv, b - 2, NP))
                act.activation(V[:, u, :, :, 0:DK], bank_y[:, :].rearrange("p (t h w) -> p t h w", t=TB, h=H),
                               ACT.Copy).then_inc(a_v, 1)

            def exps(b, p):
                act.wait_ge(a_stp, upto(a_stp, b, p + 1))
                act.wait_ge(a_pv, upto(a_pv, b, p - 1))
                act.activation(prob[:, p % 2], pair_a[:, :, P:4 * P], ACT.Exp,
                               scale=DK ** -0.5).then_inc(a_e, 1)

            def copy_o(b, h):
                act.wait_ge(a_pv, upto(a_pv, b, 4 * h + 4))
                act.wait_ge(a_ot, upto(a_ot, b - 1, h + 1))
                act.activation(oT[:, h], bank_o[:, :].rearrange("p (g t) -> p g t", g=2),
                               ACT.Copy).then_inc(a_o, 1)

            def copy_att(b):
                act.wait_ge(a_atT, upto(a_atT, b, 1))
                act.wait_ge(a_y, upto(a_y, b - 1, 1))
                act.activation(attT_hi[:, :, :], bank_t[:, :].rearrange("p (c t) -> p c t", c=CT),
                               ACT.Copy).then_inc(a_ath, 1)

            def weigh_points(b, j, u, w, second):
                if second:
                    points = range(3, WIN)
                else:
                    points = range(3)
                    if w == 0:
                        act.wait_ge(a_phi, upto(a_phi, b, 16))
                    act.wait_ge(a_sp4, upto(a_sp4, b, 3 * w))
                    act.sem_inc(passed_act, 1)
                for m in points:
                    i = act.activation(prod[:, m], basis[:, u, m], ACT.Copy, scale=cpw[:, w, bass.ds(j, 1), m])
                if second:
                    i.then_inc(a_pr, 1)

            act.wait_ge(s_const, 5)
            for b in range(2):
                copy_xT(b, b, False)
                copy_qk(b, 0, b > 0)
                copy_qk(b, 1, b > 0)
                if b == 0:
                    copy_v(0, 0)

            def period(b, j, u, prev=True, nxt=True, nxt2=True, nxt3=True):
                for p in range(NP):
                    exps(b, p)
                    if p in (1, 2, 3, 4, 6, 7):
                        weigh_points(b, j, u, (0, 0, 0, 1, 1, 2, 2, 2)[p], p in (2, 4, 7))
                    if p == 0:
                        if prev:
                            copy_o(b - 1, 1)
                        if nxt2:
                            copy_xT(b + 2, u)
                    if p == 3:
                        if prev:
                            copy_att(b - 1)
                        if nxt2:
                            copy_qk(b + 2, 0)
                    if p == 4:
                        copy_o(b, 0)
                        if nxt:
                            copy_v(b + 1, 1 - u)
                    if p == 5 and nxt2:
                        copy_qk(b + 2, 1)

            act.wait_ge(s_cp, 96)
            run_periods(act, period)
            copy_o(B - 1, 1)
            copy_att(B - 1)

            def split_spline(fills):
                for n in fills:
                    act.wait_ge(s_fturn, n + 1)
                    src = fill_bank[n % 8][:, :]
                    if n < MT:
                        dst = (wg_hi, wu_hi)[n // 4][:, :, 2 * P * (n % 4):2 * P * (n % 4) + 2 * P]
                        act.activation(dst, src.rearrange("p (c o) -> p c o", c=CT), ACT.Copy).then_inc(s_fhi, 1)
                    else:
                        cols = slice(64 * (n - MT), 64 * (n - MT) + 64)
                        for c in range(CT):
                            i = act.activation(wd_hi[:, c::CT, cols], turned_down(src)[:, c], ACT.Copy)
                        i.then_inc(s_fhi, 1)

            def ffn(f, tail):
                def high_in(g, u, h):
                    act.wait_ge(f.xT, upto(f.xT, g, h + 1))
                    act.wait_ge(f.upp, upto(f.upp, g - 2, MT))
                    act.activation(fT_hi[:, u, :, S * h:S * h + S], bank_t[:, :].rearrange("p (c t) -> p c t", c=CT),
                                   ACT.Copy).then_inc(f.xh, 1)

                def silu(g, m):
                    act.wait_ge(f.gp, upto(f.gp, g, m + 1))
                    act.wait_ge(f.up, upto(f.up, g, m - 1))
                    act.activation(gact[:, m % 2, :], pair_a[:, m % 2, :], ACT.Silu).then_inc(f.si, 1)

                def high_inner(g, m):
                    act.wait_ge(f.up, upto(f.up, g, m + 1))
                    act.wait_ge(f.dp, upto(f.dp, g, m - 1))
                    act.activation(in_hi[:, m % 2, :], inter[:, m % 2, :], ACT.Copy).then_inc(f.ih, 1)

                def period(g, u, prev=True, nxt=True):
                    for m in range(MT):
                        silu(g, m)
                        high_inner(g, m)
                        if m in (4, 5) and nxt:
                            high_in(g + 1, 1 - u, m - 4)
                        if not nxt:
                            tail(m)

                def run():
                    run_pairs(period)(act)

                return high_in, run

            def g_high_turned(n, u):
                act.wait_ge(g_.xT, upto(g_.xT, n, 1))
                act.wait_ge(g_.gi, upto(g_.gi, n - 2, 1))
                act.activation(gT_hi[:, u], bank_t[:, :].rearrange("p (c t) -> p c t", c=CT),
                               ACT.Copy).then_inc(g_.xh, 1)

            def g_high_x(n, u):
                act.wait_ge(g_.xn, upto(g_.xn, n, 2))
                act.wait_ge(g_.o, upto(g_.o, n - 2, 2))
                act.activation(val_hi[:, u, :, 0:D], gx[u], ACT.Copy).then_inc(g_.gh, 1)

            def g_norm(n, u):
                act.wait_ge(g_.mr, upto(g_.mr, n, 1))
                act.wait_ge(g_.xT, upto(g_.xT, n - 2, 1))
                act.wait_ge(g_.gl, upto(g_.gl, n - 2, 1))
                act.sem_inc(passed_act, 1)
                for t in range(TB):
                    act.activation(gx[u][:, t, :], X[:, bass.ds(TB * n + t, 1), :], ACT.Identity,
                                   bias=nmr[:, u, t:t + 1], scale=rs[:, u, t:t + 1]).then_inc(g_.xn, 1)

            def g_activate(n):
                act.wait_ge(g_.qk, upto(g_.qk, n, 1))
                act.wait_ge(g_.w, upto(g_.w, n - 1, 4))
                act.activation(kt, bank_p[0:GR, S:2 * S], ACT.Tanh, scale=0.5).then_inc(g_.kt, 1)
                act.activation(qs, bank_p[0:GR, 0:S], ACT.Silu).then_inc(g_.qs, 1)
                act.wait_ge(g_.kt, upto(g_.kt, n, 1))
                act.activation(dt, kt, ACT.Tanh, bias=quarter[0:GR, :], scale=0.25).then_inc(g_.dt, 1)
                act.activation(ks, kt, ACT.Copy, bias=0.5, scale=0.5).then_inc(g_.ks, 1)
                act.wait_ge(g_.dt, upto(g_.dt, n, 1))
                act.activation(dec, dt, ACT.Copy, bias=0.5, scale=-0.5).then_inc(g_.de, 1)

            def g_high_qk(n):
                act.wait_ge(g_.kd, upto(g_.kd, n, 1))
                act.wait_ge(g_.ap, upto(g_.ap, n - 1, 1))
                act.activation(qk_hi[:, :, :], qk, ACT.Copy).then_inc(g_.qkh, 1)

            def g_high_am(n):
                act.wait_ge(g_.am, upto(g_.am, n, 1))
                act.wait_ge(g_.o, upto(g_.o, n - 1, 2))
                act.activation(am_hi[:, :, :], am, ACT.Copy).then_inc(g_.amh, 1)

            def g_high_values(n, u):
                act.wait_ge(g_.xw, upto(g_.xw, n, 1))
                act.wait_ge(g_.o, upto(g_.o, n - 2, 2))
                act.activation(val_hi[:, u, :, D:2 * D], pair_a[:, 1, :].rearrange("p (t c) -> p t c", t=TB),
                               ACT.Copy).then_inc(g_.wh, 1)

            def g_squares(n, u):
                act.wait_ge(g_.vs, upto(g_.vs, n - 1, 1))
                for q in range(TB):
                    act.wait_ge(g_.o, upto(g_.o, n, q + 1))
                    if q:
                        act.wait_ge(g_.sq, upto(g_.sq, n, 1))
                    else:
                        act.wait_ge(g_.sq, upto(g_.sq, n - 1, 2))
                    act.activation(junk[:, :], out_bank(u, q)[:, 0:D], ACT.Square,
                                   accum_out=ssq[:, q:q + 1]).then_inc(g_.sq, 1)

            def g_gate(n, u):
                act.wait_ge(g_.mu, upto(g_.mu, n - 1, 2))
                for q in range(TB):
                    i = act.activation(gact_o[:, q, :], out_bank(u, q)[:, D:2 * D], ACT.Silu)
                i.then_inc(g_.gs, 1)

            def g_normalise(n, u):
                act.wait_ge(g_.rr, upto(g_.rr, n, 1))
                act.wait_ge(g_.res, upto(g_.res, n - 1, 1))
                for q in range(TB):
                    act.activation(rms[:, q, :], out_bank(u, q)[:, 0:D], ACT.Copy,
                                   scale=rr[:, q:q + 1]).then_inc(g_.rm, 1)

            def gla():
                g_high_values(0, 0)

                def period(n, u, prev2=True, prev=True, cur=True, nxt=True, nxt2=True, nxt3=True):
                    if prev:
                        g_high_am(n - 1)
                    if prev2:
                        g_normalise(n - 2, u)
                    if not cur:
                        f2_high(0, 0, 0)
                    if nxt2:
                        g_norm(n + 2, u)
                    if nxt:
                        g_activate(n + 1)
                    if cur:
                        g_high_qk(n)
                    if prev:
                        g_squares(n - 1, 1 - u)
                    if nxt:
                        g_high_x(n + 1, 1 - u)
                        g_high_values(n + 1, 1 - u)
                    if nxt2:
                        g_high_turned(n + 2, u)
                    if prev:
                        g_gate(n - 1, 1 - u)
                    if not cur:
                        f2_high(0, 0, 1)

                run_gla(act, period)
                g_normalise(B - 1, 1)

            def gla_start(m):
                if m == 1:
                    g_norm(0, 0)
                if m == 2:
                    g_norm(1, 1)
                if m == 3:
                    g_high_turned(0, 0)
                if m == 4:
                    g_high_x(0, 0)
                    g_activate(0)
                if m == 5:
                    g_high_turned(1, 1)

            f1_high, run_f1 = ffn(f1, gla_start)
            f2_high, run_f2 = ffn(f2, lambda m: None)
            split_spline(range(3))
            f1_high(0, 0, 0)
            split_spline(range(3, 6))
            f1_high(0, 0, 1)
            split_spline(range(6, 3 * MT // 2))
            run_f1()
            gla()
            run_f2()

        @block.vector
        def _(dve):
            rows = stack[:, 0, 0].bitcast(F32)
            dve.memset(rows, 0.0).then_inc(s_stack0, 1)
            dve.wait_ge(s_stack0, 1)
            dve.memset(rows[64:K_ST, 1], 1.0).then_inc(s_stack0, 1)
            lead(dve, by_dve + f1.dve + f2.dve + g_.dve)

            def stats(b, u):
                for t in range(TB):
                    dve.bn_stats(st[:, u, t, :], X[:, bass.ds(TB * b + t, 1), :]).then_inc(a_bn, 1)
                dve.wait_ge(a_bn, upto(a_bn, b, TB))
                dve.sem_inc(passed_dve, 1)
                for t in range(TB):
                    dve.bn_aggr(mv[:, u, t, :], st[:, u, t, :]).then_inc(a_mv, 1)
                dve.wait_ge(a_mv, upto(a_mv, b, 2))
                dve.tensor_scalar(ve[:, u, :], mv[:, u, :, 1], EPS, None, ALU.add).then_inc(a_ve, 1)

            def normalise(b, u):
                dve.wait_ge(a_rs, upto(a_rs, b, 1))
                dve.wait_ge(a_xT, upto(a_xT, b - 1, 1))
                for t in range(TB):
                    dve.tensor_scalar(xn[:, t, :], X[:, bass.ds(TB * b + t, 1), :], mv[:, u, t, 0:1],
                                      rs[:, u, t:t + 1], ALU.subtract, ALU.mult).then_inc(a_xn, 1)

            def low_weights(n):
                hi, lo = (wq, wk, wv, wo, wog, wig)[n]
                dve.wait_ge(s_prep_hi, n + 1)
                dve.tensor_tensor(lo[:, :, :], prep_bank[n][:, :].rearrange("p (c o) -> p c o", c=CT),
                                  hi[:, :, :].bitcast(F32), ALU.subtract).then_inc(s_prep_lo, 1)

            def low_gla_weights():
                dve.wait_ge(s_prep_hi, 6 + NG)
                turned = prep_bank[6][:, 0:4 * KG].rearrange("p (m k) -> p m k", k=KG)
                for g in range(NG):
                    cols = slice(KG * g, KG * g + KG)
                    i = dve.tensor_tensor(wqk_lo[:, :, :, cols].rearrange("p n c k -> p (n c) k"), turned,
                                          wqk_hi[:, :, :, cols].rearrange("p n c k -> p (n c) k").bitcast(F32),
                                          ALU.subtract)
                i.then_inc(s_prep_lo, 1)

            def low_xT(b, u, used=True):
                dve.wait_ge(a_xh, upto(a_xh, b, 1))
                if used:
                    dve.wait_ge(a_vp, upto(a_vp, b - 2, 1))
                dve.tensor_tensor(xT_lo[:, u], bank_t[:, :].rearrange("p (c t) -> p c t", c=CT),
                                  xT_hi[:, u].bitcast(F32), ALU.subtract).then_inc(a_xl, 1)

            def low_qk(b, h):
                dve.wait_ge(a_qkh, upto(a_qkh, b, h + 1))
                dve.tensor_tensor(stage[:, h, 2:0:-1, :], bank_p[:, :].rearrange("p (n t) -> p n t", n=2),
                                  stage[:, h, 0:4:3, :].bitcast(F32), ALU.subtract).then_inc(a_qkl, 1)

            def maxima(b, p, both=False):
                dve.wait_ge(a_sp, upto(a_sp, b, p + 1))
                if p % 4 == 0:
                    dve.wait_ge(a_m, upto(a_m, b - 1, 2 * (p // 4) + 2))
                h, hd = p // 4, (2 * p) % HH
                src = pair_a if both and p % 2 else pair_b
                dve.tensor_reduce(mx[:, h, hd:hd + 2, :], src[:, :, 0:3 * P].rearrange("p n (t k) -> p n t k", t=3),
                                  AX.X, ALU.max).then_inc(a_mx, 1)

            def merge_max(b, h):
                dve.wait_ge(a_mx, upto(a_mx, b, 4 * h + 4))
                dve.wait_ge(a_mT, upto(a_mT, b - 1, h + 1))
                dve.tensor_copy(mx2[:, h, 0, :], mx[:, h, :, 2]).then_inc(a_m, 1)
                dve.tensor_tensor(mx2[:, h, 1, :], mx[:, h, :, 0], mx[:, h, :, 1], ALU.max).then_inc(a_m, 1)

            def split_max(b, h):
                dve.wait_ge(a_mT, upto(a_mT, b, h + 1))
                dve.wait_ge(a_md[h], upto(a_md[h], b - 1, 32))
                dve.tensor_scalar(mrow[:, h, 0, :], bank_t[0:HH, 0:S], -1.0, None, ALU.mult).then_inc(a_mh, 1)
                dve.wait_ge(a_mh, upto(a_mh, b, h + 1))
                dve.scalar_tensor_tensor(out=mrow[:, h, 1, :], in0=bank_t[0:HH, 0:S], scalar=-1.0,
                                         in1=mrow[:, h, 0, :].bitcast(F32), op0=ALU.mult,
                                         op1=ALU.subtract).then_inc(a_ml, 1)

            def divide(b, h):
                dve.wait_ge(a_ot, upto(a_ot, b, h + 1))
                dve.wait_ge(a_at, upto(a_at, b - 1, h + 1))
                dve.reciprocal(rden[:, h], bank_y4[:, :, :, DK]).then_inc(a_rd, 1)
                dve.wait_ge(a_rd, upto(a_rd, b, h + 1))
                dve.wait_ge(a_atT, upto(a_atT, b - 1, 1))
                dst = att[:, :, P * h:P * h + P].rearrange("p t (h w) -> p t h w", w=DK)
                dve.tensor_tensor(dst, bank_y4[:, :, :, 0:DK],
                                  rden[:, h].rearrange("p t (h o) -> p t h o", o=1).to_broadcast([P, TB, HH, DK]),
                                  ALU.mult).then_inc(a_at, 1)

            def low_att(b):
                dve.wait_ge(a_ath, upto(a_ath, b, 1))
                dve.wait_ge(a_y, upto(a_y, b - 1, 1))
                dve.tensor_tensor(attT_lo[:, :, :], bank_t[:, :].rearrange("p (c t) -> p c t", c=CT),
                                  attT_hi[:, :, :].bitcast(F32), ALU.subtract).then_inc(a_atl, 1)

            def residual(b):
                dve.wait_ge(a_y, upto(a_y, b, 1))
                tok = X[:, bass.ds(TB * b, TB), :]
                dve.tensor_tensor(tok, bank_p[:, :].rearrange("p (t c) -> p t c", t=TB), tok,
                                  ALU.add).then_inc(a_res, 1)

            dve.wait_ge(s_x[0], 16)
            stats(0, 0)
            for n in range(3):
                low_weights(n)
            normalise(0, 0)
            low_weights(3)
            dve.wait_ge(s_x[1], 16)
            stats(1, 1)
            low_xT(0, 0, False)
            low_weights(4)
            low_weights(5)
            low_gla_weights()
            normalise(1, 1)
            low_qk(0, 0)
            low_qk(0, 1)
            low_xT(1, 1, False)
            low_qk(1, 0)
            for p in range(4):
                maxima(0, p, both=True)
            merge_max(0, 0)
            split_max(0, 0)
            low_qk(1, 1)
            for p in range(4, NP):
                maxima(0, p, both=True)
            merge_max(0, 1)
            dve.wait_ge(s_x[2], 16)
            stats(2, 0)
            normalise(2, 0)

            def period(b, j, u, prev=True, nxt=True, nxt2=True, nxt3=True):
                for p in range(NP):
                    if p == 0 and nxt2:
                        low_xT(b + 2, u)
                    if p == 1:
                        split_max(b, 1)
                    if p == 2 and prev:
                        divide(b - 1, 1)
                    if p == 3:
                        if prev:
                            low_att(b - 1)
                    if p == 4 and nxt3:
                        if isinstance(b, int) and b == 1:
                            dve.wait_ge(s_x[3], 16)
                        stats(b + 3, 1 - u)
                    if p == 6:
                        divide(b, 0)
                        if nxt3:
                            normalise(b + 3, 1 - u)
                    if p == 7 and prev:
                        residual(b - 1)
                    if nxt:
                        if p == 5:
                            split_max(b + 1, 0)
                        maxima(b + 1, p)
                        if p == 3:
                            merge_max(b + 1, 0)
                        if p == 7:
                            merge_max(b + 1, 1)
                    if nxt2 and p in (3, 5):
                        low_qk(b + 2, p // 4)

            run_periods(dve, period)
            def split_spline(fills):
                for n in fills:
                    dve.wait_ge(s_fhi, n + 1)
                    src = fill_bank[n % 8][:, :]
                    if n < MT:
                        cols = slice(2 * P * (n % 4), 2 * P * (n % 4) + 2 * P)
                        hi, lo = ((wg_hi, wg_lo), (wu_hi, wu_lo))[n // 4]
                        i = dve.tensor_tensor(lo[:, :, cols], src.rearrange("p (c o) -> p c o", c=CT),
                                              hi[:, :, cols].bitcast(F32), ALU.subtract)
                    else:
                        cols = slice(64 * (n - MT), 64 * (n - MT) + 64)
                        for c in range(CT):
                            i = dve.tensor_tensor(wd_lo[:, c::CT, cols], turned_down(src)[:, c],
                                                  wd_hi[:, c::CT, cols].bitcast(F32), ALU.subtract)
                    i.then_inc(s_flo, 1)

            def ffn(f, tail):
                def stats4(g):
                    for t in range(2 * TB):
                        dve.bn_stats(st[:, t // TB, t % TB, :],
                                     X[:, bass.ds(2 * TB * g + t, 1), :]).then_inc(f.bn, 1)
                    dve.wait_ge(f.bn, upto(f.bn, g, 4))
                    dve.sem_inc(passed_dve, 1)
                    for t in range(2 * TB):
                        dve.bn_aggr(mv[:, t // TB, t % TB, :], st[:, t // TB, t % TB, :]).then_inc(f.mv, 1)
                    dve.wait_ge(f.mv, upto(f.mv, g, 4))
                    dve.tensor_scalar(ve[:, :, :], mv[:, :, :, 1], EPS, None, ALU.add).then_inc(f.ve, 1)

                def normalise4(g, tiles):
                    dve.wait_ge(f.rs, upto(f.rs, g, 1))
                    dve.wait_ge(f.xT, upto(f.xT, g - 1, 2))
                    for t in tiles:
                        dve.tensor_scalar(xn_f[:, t, :], X[:, bass.ds(2 * TB * g + t, 1), :],
                                          mv[:, t // TB, t % TB, 0:1], rs[:, t // TB, t % TB:t % TB + 1],
                                          ALU.subtract, ALU.mult).then_inc(f.xn, 1)

                def low_in(g, u, h):
                    dve.wait_ge(f.xh, upto(f.xh, g, h + 1))
                    dve.wait_ge(f.upp, upto(f.upp, g - 2, MT))
                    dst = slice(S * h, S * h + S)
                    dve.tensor_tensor(fT_lo[:, u, :, dst], bank_t[:, :].rearrange("p (c t) -> p c t", c=CT),
                                      fT_hi[:, u, :, dst].bitcast(F32), ALU.subtract).then_inc(f.xl, 1)

                def gated(g, m):
                    dve.wait_ge(f.upp, upto(f.upp, g, m + 1))
                    dve.wait_ge(f.si, upto(f.si, g, m + 1))
                    dve.wait_ge(f.ih, upto(f.ih, g, m - 1))
                    dve.tensor_tensor(inter[:, m % 2, :], gact[:, m % 2, :], pair_b[:, m % 2, :],
                                      ALU.mult).then_inc(f.up, 1)

                def low_inner(g, m):
                    dve.wait_ge(f.ih, upto(f.ih, g, m + 1))
                    dve.tensor_tensor(in_lo[:, m % 2, :], inter[:, m % 2, :], in_hi[:, m % 2, :].bitcast(F32),
                                      ALU.subtract).then_inc(f.il, 1)

                def residual2(g, h):
                    dve.wait_ge(f.dp, upto(f.dp, g, MT))
                    tok = X[:, bass.ds(2 * TB * g + TB * h, TB), :]
                    dve.tensor_tensor(tok, (bank_o, bank_y)[h][:, :].rearrange("p (t c) -> p t c", t=TB), tok,
                                      ALU.add).then_inc(f.res, 1)

                def period(g, u, prev=True, nxt=True):
                    for m in range(MT):
                        gated(g, m)
                        low_inner(g, m)
                        if m == 0 and prev:
                            residual2(g - 1, 0)
                            residual2(g - 1, 1)
                        if m == 1 and nxt:
                            stats4(g + 1)
                        if m in (2, 3) and nxt:
                            normalise4(g + 1, range(TB * (m - 2), TB * (m - 1)))
                        if m in (4, 5) and nxt:
                            low_in(g + 1, 1 - u, m - 4)
                        if not nxt:
                            tail(m)

                def run():
                    run_pairs(period)(dve)
                    residual2(PAIRS - 1, 0)
                    residual2(PAIRS - 1, 1)

                return stats4, normalise4, low_in, run

            def g_stats(n, u):
                for t in range(TB):
                    dve.bn_stats(st[:, u, t, :], X[:, bass.ds(TB * n + t, 1), :]).then_inc(g_.bn, 1)
                dve.wait_ge(g_.bn, upto(g_.bn, n, TB))
                dve.sem_inc(passed_dve, 1)
                for t in range(TB):
                    dve.bn_aggr(mv[:, u, t, :], st[:, u, t, :]).then_inc(g_.mv, 1)
                dve.wait_ge(g_.mv, upto(g_.mv, n, TB))
                dve.tensor_scalar(negm[:, u, :], mv[:, u, :, 0], -1.0, None, ALU.mult).then_inc(g_.nm, 1)
                dve.tensor_scalar(ve[:, u, :], mv[:, u, :, 1], EPS, None, ALU.add).then_inc(g_.ve, 1)

            def g_low_turned(n, u):
                dve.wait_ge(g_.xh, upto(g_.xh, n, 1))
                dve.wait_ge(g_.gi, upto(g_.gi, n - 2, 1))
                dve.tensor_tensor(gT_lo[:, u], bank_t[:, :].rearrange("p (c t) -> p c t", c=CT),
                                  gT_hi[:, u].bitcast(F32), ALU.subtract).then_inc(g_.xl, 1)

            def g_scans(n):
                dve.wait_ge(g_.w, upto(g_.w, n, 4))
                dve.wait_ge(g_.qd, upto(g_.qd, n - 1, 1))
                dve.tensor_tensor_scan(fq, dq, win[:, 1], 0.0, ALU.mult, ALU.add).then_inc(g_.sf, 1)
                dve.tensor_tensor_scan(fk[64:GR, ::-1], dk[64:GR, ::-1], win[64:GR, 3, ::-1], 0.0, ALU.mult,
                                       ALU.add).then_inc(g_.sb, 1)

            def g_decayed(n):
                dve.wait_ge(g_.sf, upto(g_.sf, n, 1))
                dve.reciprocal(fk[0:64], fq[0:64]).then_inc(g_.rc, 1)
                dve.wait_ge(g_.qkh, upto(g_.qkh, n - 1, 1))
                dve.tensor_tensor(qk[:, 0], qwn, fq, ALU.mult).then_inc(g_.qd, 1)
                dve.wait_ge(g_.rc, upto(g_.rc, n, 1))
                dve.tensor_tensor(qk[:, 1], kwn, fk, ALU.mult).then_inc(g_.kd, 1)

            def g_low_qk(n):
                dve.wait_ge(g_.qkh, upto(g_.qkh, n, 1))
                dve.tensor_tensor(qk_lo[:, :, :], qk, qk_hi[:, :, :].bitcast(F32), ALU.subtract).then_inc(g_.qkl, 1)

            def g_masked(n):
                dve.wait_ge(g_.ap, upto(g_.ap, n, 1))
                dve.wait_ge(g_.amh, upto(g_.amh, n - 1, 1))
                dve.scalar_tensor_tensor(out=am, in0=pair_a[:, 0, :].rearrange("p (k t) -> p k t", k=TB), scalar=BIG,
                                         in1=causal01[:, :, :], op0=ALU.min, op1=ALU.mult).then_inc(g_.am, 1)

            def g_low_am(n):
                dve.wait_ge(g_.amh, upto(g_.amh, n, 1))
                dve.tensor_tensor(am_lo[:, :, :], am, am_hi[:, :, :].bitcast(F32), ALU.subtract).then_inc(g_.aml, 1)

            def g_low_values(n, u):
                dve.wait_ge(g_.wh, upto(g_.wh, n, 1))
                dve.tensor_tensor(val_lo[:, u, :, D:2 * D], pair_a[:, 1, :].rearrange("p (t c) -> p t c", t=TB),
                                  val_hi[:, u, :, D:2 * D].bitcast(F32), ALU.subtract).then_inc(g_.wl, 1)

            def g_mean_square(n):
                dve.wait_ge(g_.sq, upto(g_.sq, n, 2))
                dve.wait_ge(g_.rr, upto(g_.rr, n - 1, 1))
                dve.tensor_scalar(vs[:, :], ssq[:, :], 1.0 / D, EPS, ALU.mult, ALU.add).then_inc(g_.vs, 1)

            def gla():
                dve.wait_ge(s_gload, 32)
                dve.wait_ge(s_gc, 4)
                g_low_values(0, 0)
                dve.wait_ge(f1.res, upto(f1.res, PAIRS - 1, 2))

                def period(n, u, prev2=True, prev=True, cur=True, nxt=True, nxt2=True, nxt3=True):
                    if prev:
                        g_masked(n - 1)
                    if cur:
                        g_scans(n)
                    if prev:
                        g_low_am(n - 1)
                    if nxt3:
                        g_stats(n + 3, 1 - u)
                    if cur:
                        g_decayed(n)
                        g_low_qk(n)
                    if prev:
                        g_mean_square(n - 1)
                    if nxt:
                        g_low_values(n + 1, 1 - u)
                    if nxt2:
                        g_low_turned(n + 2, u)
                    if nxt and not nxt2:
                        dve.wait_ge(g_.xn, upto(g_.xn, B - 1, 2))
                        dve.wait_ge(g_.res, upto(g_.res, 1, 1))
                        f2_stats(0)
                    if cur and not nxt:
                        f2_normalise(0, range(2 * TB))
                    if not cur:
                        f2_low(0, 0, 0)
                        f2_low(0, 0, 1)

                run_gla(dve, period)

            def gla_start(m):
                if m == 0:
                    dve.wait_ge(f1.res, upto(f1.res, 1, 2))
                    g_stats(0, 0)
                if m == 1:
                    g_stats(1, 1)
                if m == 2:
                    dve.wait_ge(g_.xn, upto(g_.xn, 0, 2))
                    g_stats(2, 0)
                if m == 3:
                    g_low_turned(0, 0)
                if m == 5:
                    g_low_turned(1, 1)

            f1_stats, f1_normalise, f1_low, run_f1 = ffn(f1, gla_start)
            f2_stats, f2_normalise, f2_low, run_f2 = ffn(f2, lambda m: None)
            dve.wait_ge(a_res, upto(a_res, 1, 1))
            f1_stats(0)
            divide(B - 1, 1)
            low_att(B - 1)
            residual(B - 1)
            dve.wait_ge(a_sp4, upto(a_sp4, B - 1, 9))
            f1_normalise(0, range(2 * TB))
            split_spline(range(3))
            f1_low(0, 0, 0)
            split_spline(range(3, 6))
            f1_low(0, 0, 1)
            split_spline(range(6, 3 * MT // 2))
            dve.wait_ge(a_res, upto(a_res, B - 1, 1))
            run_f1()
            gla()
            dve.wait_ge(g_.res, upto(g_.res, B - 1, 1))
            run_f2()


def kernel(**inputs):
    import concourse.bacc as bacc
    from concourse.bass_utils import run_bass_kernel_spmd

    arrays = {}
    for name, value in inputs.items():
        if not name.endswith("_cp"):
            arrays[name.replace("L0_", "in_")] = np.ascontiguousarray(value)
    cps = np.zeros((3, N_CP), np.float32)
    for n, name in enumerate(("gate", "up", "down")):
        cps[n, FRONT:FRONT + N_CTRL] = inputs[f"L0_ffn_{name}_cp"]
    arrays["control_points"] = cps
    arrays["spline_basis"] = spline_basis()
    arrays["decay_windows"] = decay_windows()
    nc = bacc.Bacc("TRN2", target_bir_lowering=False, num_devices=1)
    args = [nc.dram_tensor(n, a.shape, mybir.dt.from_np(a.dtype), kind="ExternalInput").ap()
            for n, a in arrays.items()]
    result = nc.dram_tensor("result", (B, S, D), F32, kind="ExternalOutput").ap()
    build(nc, *args, result)
    return run_bass_kernel_spmd(nc, [arrays], core_ids=[0]).results[0]["result"]
```
